# Optimizing a Trainium2 kernel written in Bass

```python
import numpy as np
import jax
import jax.numpy as jnp

def _softmax(x, axis=-1):
    return jax.nn.softmax(x, axis=axis)

def _gelu(x):
    return jax.nn.gelu(x, approximate=True)

def _silu(x):
    return jax.nn.silu(x)

def _sigmoid(x):
    return jax.nn.sigmoid(x)

def _layernorm(x, axis=-1, eps=1e-05):
    m = jnp.mean(x, axis=axis, keepdims=True)
    v = jnp.var(x, axis=axis, keepdims=True)
    return (x - m) / jnp.sqrt(v + eps)

def _scatter_add(tgt, idx, src, axis=0):
    return tgt.at[idx].add(src)

def _segment_sum(src, seg, n):
    return jax.ops.segment_sum(src, seg, n)
kernel_name = 'mk_rec_standalone_d1_rec_r8_0b1541'

def setup_inputs(seed: int=0):
    np.random.seed(seed)
    _w = jnp.asarray

    def _rec_inputs():
        import jax
        import jax.numpy as jnp
        _rk = jax.random.key(seed)
        r_wfts = jax.random.bernoulli(jax.random.fold_in(_rk, 1), 0.0007515, (1024, 5120)).astype(jnp.float32)
        r_bfts = jax.random.bernoulli(jax.random.fold_in(_rk, 2), 0.0007509, (1024, 5120)).astype(jnp.float32)
        r_stm = jax.random.bernoulli(jax.random.fold_in(_rk, 3), 0.4937, (1024, 1)).astype(jnp.float32)
        return (r_wfts, r_bfts, r_stm)
    r_wfts, r_bfts, r_stm = _rec_inputs()

    def _L0_rec_setup():
        import jax, jax.numpy as jnp
        import numpy as np
        NUM_FEATURES = 5120
        FT_OUT = 257
        B = 512

        def crelu(x):
            return jnp.clip(x, 0.0, 1.0)
        key = jax.random.key(seed)
        ks = jax.random.split(key, 12)
        inp = {'wfts': (jax.random.uniform(ks[0], (B, NUM_FEATURES)) < 0.00075).astype(jnp.float32), 'bfts': (jax.random.uniform(ks[1], (B, NUM_FEATURES)) < 0.00075).astype(jnp.float32), 'stm': (jax.random.uniform(ks[2], (B, 1)) < 0.5).astype(jnp.float32), 'ft_w': jax.random.normal(ks[3], (FT_OUT, NUM_FEATURES)) * 0.01, 'ft_b': jax.random.normal(ks[4], (FT_OUT,)) * 0.01, 'l1_w': jax.random.normal(ks[5], (32, 512)) * 0.05, 'l1_b': jax.random.normal(ks[6], (32,)) * 0.05, 'l2_w': jax.random.normal(ks[7], (32, 32)) * 0.1, 'l2_b': jax.random.normal(ks[8], (32,)) * 0.1, 'l3_w': jax.random.normal(ks[9], (1, 32)) * 0.1, 'l3_b': jax.random.normal(ks[10], (1,)) * 0.1}
        return inp
    _L0_rec_all = _L0_rec_setup()
    _L0_rec_in = {k: v for k, v in _L0_rec_all.items() if k in ('ft_w', 'ft_b', 'l1_w', 'l1_b', 'l2_w', 'l2_b', 'l3_w', 'l3_b')}
    del _L0_rec_all
    return {'r_wfts': r_wfts, 'r_bfts': r_bfts, 'r_stm': r_stm, 'L0_rec_ft_w': _L0_rec_in['ft_w'], 'L0_rec_ft_b': _L0_rec_in['ft_b'], 'L0_rec_l1_w': _L0_rec_in['l1_w'], 'L0_rec_l1_b': _L0_rec_in['l1_b'], 'L0_rec_l2_w': _L0_rec_in['l2_w'], 'L0_rec_l2_b': _L0_rec_in['l2_b'], 'L0_rec_l3_w': _L0_rec_in['l3_w'], 'L0_rec_l3_b': _L0_rec_in['l3_b']}

def reference(r_wfts, r_bfts, r_stm, L0_rec_ft_w, L0_rec_ft_b, L0_rec_l1_w, L0_rec_l1_b, L0_rec_l2_w, L0_rec_l2_b, L0_rec_l3_w, L0_rec_l3_b):
    import jax
    import jax.numpy as jnp

    def _L0_rec_ref(wfts, bfts, stm, ft_w, ft_b, l1_w, l1_b, l2_w, l2_b, l3_w, l3_b):
        import jax, jax.numpy as jnp
        import numpy as np
        NUM_FEATURES = 5120
        FT_OUT = 257
        B = 512

        def crelu(x):
            return jnp.clip(x, 0.0, 1.0)
        wp = wfts @ ft_w.T + ft_b
        bp = bfts @ ft_w.T + ft_b
        w, wpsqt = (wp[:, :FT_OUT - 1], wp[:, FT_OUT - 1:])
        b, bpsqt = (bp[:, :FT_OUT - 1], bp[:, FT_OUT - 1:])
        acc = stm * jnp.concatenate([w, b], axis=1) + (1.0 - stm) * jnp.concatenate([b, w], axis=1)
        x = crelu(acc)
        x = crelu(x @ l1_w.T + l1_b)
        x = crelu(x @ l2_w.T + l2_b)
        x = x @ l3_w.T + l3_b
        return x + (wpsqt + bpsqt) * (stm - 0.5)
    y = _L0_rec_ref(r_wfts, r_bfts, r_stm, L0_rec_ft_w, L0_rec_ft_b, L0_rec_l1_w, L0_rec_l1_b, L0_rec_l2_w, L0_rec_l2_b, L0_rec_l3_w, L0_rec_l3_b)
    return y

_drawn_inputs = setup_inputs


def setup_inputs(seed=0):
    import zlib

    import numpy as np

    out = dict(_drawn_inputs(seed))
    spreads = {}
    factors = {}
    for name, (base, spread) in spreads.items():
        noise = np.random.default_rng([zlib.crc32(name.encode()), seed]).standard_normal(out[name].shape)
        drawn = base * np.exp(spread * noise) if base else spread * noise
        out[name] = jnp.asarray(drawn.astype(out[name].dtype))
    for name, factor in factors.items():
        out[name] = (out[name] * factor).astype(out[name].dtype)
    return out
```

```python
from contextlib import ExitStack

import concourse.bass as bass
from concourse import mybir

F32 = mybir.dt.float32
F32R = mybir.dt.float32r
BF16 = mybir.dt.bfloat16
U16 = mybir.dt.uint16
U8 = mybir.dt.uint8
I32 = mybir.dt.int32
ALU = mybir.AluOpType
ACT = mybir.ActivationFunctionType
AXIS_X = mybir.AxisListType.X

P = 128
BATCH = 1024
FEATURES = 5120
HALF = 256
MT = HALF // P
HID = 32
KC = 5
NCH = FEATURES // (P * KC)
NK = KC * NCH
COLS = 512
PSQ_TILES = 4
PSQ_M = 32

PIECES = [(512, 0, 2), (256, 512, 1), (256, 768, 1)]
FIRST_SLOT = [0, 2 * NCH, 3 * NCH]
SLOTS = 4 * NCH
RING = 4
W_RING = 2

C_FTB = 0
C_W1 = C_FTB + MT
C_B1 = C_W1 + 2 * MT * HID
C_W2 = C_B1 + HID
C_W3 = C_W2 + HID
C_BP = C_W3 + 1
C_WP = C_BP + 1
C_ALL = C_WP + NK


def build(nc, x, w, consts, stm, out):
    with ExitStack() as ctx:
        def sb(name, shape, dt):
            return ctx.enter_context(nc.sbuf_tensor(name, shape, dt))

        def sem(name):
            return ctx.enter_context(nc.semaphore(name))

        w_hi = sb("w_hi", [P, NK, HALF], F32R)
        w_lo = sb("w_lo", [P, NK, HALF], F32R)
        w_raw = sb("w_raw", [P, W_RING, KC, HALF], F32)
        x_raw = sb("x_raw", [P, RING, KC, COLS], F32)
        x_cast = sb("x_cast", [P, RING, KC, COLS], F32R)
        low_bits = sb("low_bits", [P, KC, COLS], U8)
        low_sums = sb("low_sums", [P, SLOTS], F32)
        low_sum = sb("low_sum", [P, 1], F32)
        flag = sb("flag", [1, 1], I32)
        con = sb("con", [P, C_ALL], F32)
        psq_w = sb("psq_w", [P, NK, PSQ_M], BF16)
        psq_rest = sb("psq_rest", [P, 2, NK], F32)
        psq_bias = sb("psq_bias", [P, 1], F32)
        psq_slow = sb("psq_slow", [P, KC], F32)
        ones = sb("ones", [P, COLS], F32)
        side = sb("side", [P, BATCH], F32)
        black = sb("black", [P, MT, COLS], F32)
        diff = sb("diff", [P, COLS], F32)
        moved = sb("moved", [P, COLS], F32)
        hidden0 = sb("hidden0", [P, 2 * MT, COLS], F32)
        psq = sb("psq", [P, COLS], F32)
        hidden1 = sb("hidden1", [HID + 1, COLS], F32)
        hidden2 = sb("hidden2", [HID + 1, COLS], F32)
        y = sb("y", [1, COLS], F32)
        bank = [ctx.enter_context(nc.psum_tensor(f"bank{i}", [P, COLS], F32)) for i in range(8)]

        L1_BANK, L2_BANK, Y_BANK, FLAG_BANK = bank[2], bank[3], bank[2], bank[5]
        PSQ_BANK = [bank[6], bank[7], bank[6]]

        def accumulators(piece, m):
            if piece == 0:
                return bank[2 * m][:, :], bank[2 * m + 1][:, :]
            n = PIECES[piece][0]
            b = bank[(4, 0)[piece - 1] + m]
            return b[:, 0:n], b[:, n:2 * n]

        con_landed = sem("con_landed")
        side_landed = sem("side_landed")
        x_landed = [sem(f"x_landed{j}") for j in range(RING)]
        w_landed = [sem(f"w_landed{j}") for j in range(W_RING)]
        ones_set = sem("ones_set")
        setup_step = sem("setup_step")
        psq_w_ready = sem("psq_w_ready")
        side_ready = sem("side_ready")
        hi_ready = sem("hi_ready")
        lo_ready = sem("lo_ready")
        cast_ready = sem("cast_ready")
        low_checked = sem("low_checked")
        psq_taken = sem("psq_taken")
        main_done = sem("main_done")
        acc_ready = [sem(f"acc_ready{m}") for m in range(MT)]
        psq_acc_ready = sem("psq_acc_ready")
        black_ready = sem("black_ready")
        mix_step = sem("mix_step")
        hidden0_ready = sem("hidden0_ready")
        psq_ready = sem("psq_ready")
        l1_done = sem("l1_done")
        hidden1_ready = sem("hidden1_ready")
        l2_done = sem("l2_done")
        hidden2_ready = sem("hidden2_ready")
        y_done = sem("y_done")
        y_ready = sem("y_ready")
        out_landed = sem("out_landed")
        low_sum_ready = sem("low_sum_ready")
        flag_sum_ready = sem("flag_sum_ready")
        flag_ready = sem("flag_ready")
        g_landed = sem("g_landed")
        g_zeroed = sem("g_zeroed")
        g_psq_w_ready = sem("g_psq_w_ready")
        g_chunk_done = sem("g_chunk_done")


        def act_black(act, piece, t):
            n = PIECES[piece][0]
            for m in range(MT):
                act.wait_ge(acc_ready[m], t)
                if t > 1:
                    act.wait_ge(hidden0_ready, 2 * MT * (t - 1))
                nc.scalar.activation(black[:, m, 0:n], accumulators(piece, m)[1], ACT.Identity,
                                     bias=con[:, C_FTB + m:C_FTB + m + 1]).then_inc(black_ready, 1)

        def act_output(act, piece, t):
            n, row, _ = PIECES[piece]
            act.wait_ge(y_done, t)
            if t > 1:
                act.wait_ge(out_landed, 16 * (t - 1))
            nc.scalar.copy(y[:, 0:n], Y_BANK[0:1, 0:n]).then_inc(y_ready, 1)
            act.wait_ge(y_ready, t)
            act.dma_start(out[row:row + n].rearrange("n a -> a n"), y[:, 0:n]).then_inc(out_landed, 16)

        def dve_mix(dve, piece, t, m):
            n, row, _ = PIECES[piece]
            white = accumulators(piece, m)[0]
            bias = con[:, C_FTB + m:C_FTB + m + 1]
            step = 5 * (MT * (t - 1) + m)
            dve.wait_ge(acc_ready[m], t)
            dve.wait_ge(black_ready, MT * (t - 1) + m + 1)
            nc.vector.scalar_tensor_tensor(diff[:, 0:n], white, bias, black[:, m, 0:n],
                                           ALU.add, ALU.subtract).then_inc(mix_step, 1)
            dve.wait_ge(mix_step, step + 1)
            if t == 1:
                dve.wait_ge(side_landed, 16)
            nc.vector.tensor_tensor(moved[:, 0:n], diff[:, 0:n], side[:, row:row + n],
                                    ALU.mult).then_inc(mix_step, 1)
            dve.wait_ge(mix_step, step + 2)
            if t > 1:
                dve.wait_ge(l1_done, t - 1)
            nc.vector.tensor_tensor(hidden0[:, m, 0:n], black[:, m, 0:n], moved[:, 0:n],
                                    ALU.add).then_inc(mix_step, 1)
            nc.vector.scalar_tensor_tensor(hidden0[:, MT + m, 0:n], white, bias, moved[:, 0:n],
                                           ALU.add, ALU.subtract).then_inc(mix_step, 1)
            dve.wait_ge(mix_step, step + 3)
            nc.vector.tensor_scalar(hidden0[:, m, 0:n], hidden0[:, m, 0:n], 0.0, 1.0,
                                    ALU.max, ALU.min).then_inc(hidden0_ready, 1)
            dve.wait_ge(mix_step, step + 4)
            nc.vector.tensor_scalar(hidden0[:, MT + m, 0:n], hidden0[:, MT + m, 0:n], 0.0, 1.0,
                                    ALU.max, ALU.min).then_inc(hidden0_ready, 1)
            dve.sem_inc(mix_step, 1)

        def dve_psq(dve, piece, t):
            n, row, _ = PIECES[piece]
            dve.wait_ge(psq_acc_ready, t)
            if t == 1:
                dve.wait_ge(side_landed, 16)
            if t > 1:
                dve.wait_ge(y_done, t - 1)
            nc.vector.tensor_scalar(psq[:, 0:n], side[:, row:row + n], 0.5, None, ALU.subtract).then_inc(side_ready, 1)
            dve.wait_ge(side_ready, t)
            nc.vector.scalar_tensor_tensor(psq[:, 0:n], PSQ_BANK[piece][:, 0:n], psq_bias[:, 0:1],
                                           psq[:, 0:n],
                                           ALU.add, ALU.mult).then_inc(psq_ready, 1)

        def dve_hidden1(dve, piece, t):
            n = PIECES[piece][0]
            dve.wait_ge(l1_done, t)
            nc.vector.tensor_scalar(hidden1[0:HID, 0:n], L1_BANK[0:HID, 0:n], 0.0, 1.0,
                                    ALU.max, ALU.min).then_inc(hidden1_ready, 1)

        def dve_hidden2(dve, piece, t):
            n = PIECES[piece][0]
            dve.wait_ge(l2_done, t)
            nc.vector.tensor_scalar(hidden2[0:HID, 0:n], L2_BANK[0:HID, 0:n], 0.0, 1.0,
                                    ALU.max, ALU.min).then_inc(hidden2_ready, 1)

        def pe_l1(pe, piece, t):
            n = PIECES[piece][0]
            pe.wait_ge(hidden0_ready, 2 * MT * t)
            if t > 1:
                pe.wait_ge(y_ready, t - 1)
            nc.tensor.matmul(L1_BANK[0:HID, 0:n], con[0:1, C_B1:C_B1 + HID], ones[0:1, 0:n],
                             start=True, stop=False)
            for i in range(2 * MT):
                last = nc.tensor.matmul(L1_BANK[0:HID, 0:n], con[:, C_W1 + i * HID:C_W1 + (i + 1) * HID],
                                        hidden0[:, i, 0:n], start=False, stop=(i == 2 * MT - 1))
            last.then_inc(l1_done, 1)

        def pe_l2(pe, piece, t):
            n = PIECES[piece][0]
            pe.wait_ge(hidden1_ready, t)
            nc.tensor.matmul(L2_BANK[0:HID, 0:n], con[0:HID + 1, C_W2:C_W2 + HID], hidden1[:, 0:n],
                             start=True, stop=True).then_inc(l2_done, 1)

        def pe_l3(pe, piece, t):
            n = PIECES[piece][0]
            pe.wait_ge(psq_ready, t)
            nc.tensor.matmul(Y_BANK[0:1, 0:n], ones[:, 0:1], psq[:, 0:n], start=True, stop=False)
            pe.wait_ge(hidden2_ready, t)
            nc.tensor.matmul(Y_BANK[0:1, 0:n], con[0:HID + 1, C_W3:C_W3 + 1], hidden2[:, 0:n],
                             start=False, stop=True).then_inc(y_done, 1)

        block = ctx.enter_context(nc.Block())

        @block.sync
        def _(sp):
            def load_weights(c, j, first):
                if not first:
                    sp.wait_ge(hi_ready, c - W_RING + 1)
                    sp.wait_ge(lo_ready, c - W_RING + 1)
                sp.dma_start(w_raw[:, j], w[c]).then_inc(w_landed[j], 16)

            def load_slot(s, j, first):
                if not first:
                    sp.wait_ge(psq_taken, s - RING + 1)
                    sp.wait_ge(cast_ready, s - RING + 1)
                    sp.wait_ge(low_checked, s - RING + 1)
                sp.dma_start(x_raw[:, j], x[s]).then_inc(x_landed[j], 16)

            sp.dma_start(con[:, :], consts).then_inc(con_landed, 16)
            for j in range(RING):
                if j % 2 == 0:
                    load_weights(j // 2, j // 2, True)
                load_slot(j, j, True)
            sp.dma_start(side[:, :], stm.partition_broadcast(P)).then_inc(side_landed, 16)
            with sp.Fori(1, 2 * NCH // RING) as i:
                for j in range(RING):
                    if j % 2 == 0:
                        load_weights(i * W_RING + j // 2, j // 2, False)
                    load_slot(i * RING + j, j, False)
            with sp.Fori(2 * NCH // RING, SLOTS // RING) as i:
                for j in range(RING):
                    load_slot(i * RING + j, j, False)

            sp.wait_ge(flag_ready, 1)
            general = sp.value_load(flag[0:1, 0:1], min_val=0, max_val=1)
            sp.wait_ge(out_landed, 16 * len(PIECES))
            with sp.If(general == 1):
                sp.wait_ge(psq_taken, SLOTS)
                sp.wait_ge(cast_ready, SLOTS)
                sp.wait_ge(low_checked, SLOTS)
                sp.wait_ge(hi_ready, NCH)
                sp.wait_ge(lo_ready, NCH)
                for piece, (_, _, per) in enumerate(PIECES):
                    with sp.Fori(0, NCH) as c:
                        sp.wait_ge(g_chunk_done, c + (NCH * piece + 1))
                        sp.dma_start(w_raw[:, 0], w[c]).then_inc(g_landed, 16)
                        for j in range(per):
                            sp.dma_start(x_raw[:, j], x[c * per + (FIRST_SLOT[piece] + j)]).then_inc(g_landed, 16)
                sp.wait_ge(out_landed, 2 * 16 * len(PIECES))

        @block.gpsimd
        def _(pool):
            nc.gpsimd.memset(ones[:, :], 1.0).then_inc(ones_set, 1)
            pool.wait_ge(ones_set, 1)
            nc.gpsimd.memset(hidden1[HID:HID + 1, :], 1.0).then_inc(ones_set, 1)
            pool.wait_ge(ones_set, 2)
            nc.gpsimd.memset(hidden2[HID:HID + 1, :], 1.0).then_inc(ones_set, 1)

        @block.scalar
        def _(act):
            def hi_part(c, j, i):
                act.wait_ge(w_landed[j], i * 16 + 16)
                nc.scalar.copy(w_hi[:, bass.ds(c * KC, KC), :], w_raw[:, j]).then_inc(hi_ready, 1)

            def check_low_bits(s, j, i, first):
                act.wait_ge(x_landed[j], i * 16 + 16)
                if not first:
                    act.wait_ge(low_checked, s)
                bits = x_raw[:, j].bitcast(U16).rearrange("p k (n h) -> p k n h", h=2)[:, :, :, 0]
                nc.scalar.activation(low_bits[:, :, :], bits, ACT.Copy,
                                     accum_out=low_sums[:, bass.ds(s, 1)]).then_inc(low_checked, 1)

            for j in range(RING):
                if j % 2 == 0:
                    hi_part(j // 2, j // 2, 0)
                check_low_bits(j, j, 0, j == 0)
            with act.Fori(1, 2 * NCH // RING) as i:
                for j in range(RING):
                    if j % 2 == 0:
                        hi_part(i * W_RING + j // 2, j // 2, i)
                    check_low_bits(i * RING + j, j, i, False)
            for s in range(2 * NCH, SLOTS):
                for piece in (0, 1):
                    if s == FIRST_SLOT[piece + 1] + 3:
                        act_black(act, piece, piece + 1)
                    if s == FIRST_SLOT[piece + 1] + 7:
                        act_output(act, piece, piece + 1)
                check_low_bits(s, s % RING, s // RING, False)
            act_black(act, 2, 3)
            act_output(act, 2, 3)

            act.wait_ge(flag_ready, 1)
            general = act.value_load(flag[0:1, 0:1], min_val=0, max_val=1)
            with act.If(general == 1):
                for piece in range(len(PIECES)):
                    act_black(act, piece, len(PIECES) + piece + 1)
                    act_output(act, piece, len(PIECES) + piece + 1)

        @block.vector
        def _(dve):
            nc.vector.memset(psq_w[:, :, :], 0.0).then_inc(setup_step, 1)
            dve.wait_ge(con_landed, 16)
            nc.vector.tensor_scalar(psq_bias[:, :], con[:, C_BP:C_BP + 1], 2.0, None,
                                    ALU.mult).then_inc(psq_w_ready, 1)
            wp = con[:, C_WP:C_WP + NK]
            dve.wait_ge(setup_step, 1)
            nc.vector.tensor_copy(psq_w[:, :, 0], wp).then_inc(setup_step, 1)
            dve.wait_ge(setup_step, 2)
            nc.vector.tensor_tensor(psq_rest[:, 0, :], wp, psq_w[:, :, 0], ALU.subtract).then_inc(setup_step, 1)
            dve.wait_ge(setup_step, 3)
            nc.vector.tensor_copy(psq_w[:, :, 1], psq_rest[:, 0, :]).then_inc(setup_step, 1)
            dve.wait_ge(setup_step, 4)
            nc.vector.tensor_tensor(psq_rest[:, 1, :], psq_rest[:, 0, :], psq_w[:, :, 1],
                                    ALU.subtract).then_inc(setup_step, 1)
            dve.wait_ge(setup_step, 5)
            nc.vector.tensor_copy(psq_w[:, :, 2], psq_rest[:, 1, :]).then_inc(psq_w_ready, 1)

            def lo_part(c, j):
                dve.wait_ge(hi_ready, c + 1)
                nc.vector.tensor_tensor(w_lo[:, bass.ds(c * KC, KC), :], w_raw[:, j],
                                        w_hi[:, bass.ds(c * KC, KC), :].bitcast(F32),
                                        ALU.subtract).then_inc(lo_ready, 1)

            def cast_slot(s, j, i, first):
                dve.wait_ge(x_landed[j], i * 16 + 16)
                if not first:
                    dve.wait_ge(main_done, s - RING + 1)
                nc.vector.tensor_copy(x_cast[:, j], x_raw[:, j]).then_inc(cast_ready, 1)

            for j in range(RING):
                cast_slot(j, j, 0, True)
                if j % 2 == 0:
                    lo_part(j // 2, j // 2)
            with dve.Fori(1, 2 * NCH // RING) as i:
                for j in range(RING):
                    if j % 2 == 0:
                        lo_part(i * W_RING + j // 2, j // 2)
                    cast_slot(i * RING + j, j, i, False)
            for s in range(2 * NCH, SLOTS):
                for piece in (0, 1):
                    if s == FIRST_SLOT[piece + 1] + 3:
                        dve_mix(dve, piece, piece + 1, 0)
                    if s == FIRST_SLOT[piece + 1] + 4:
                        dve_mix(dve, piece, piece + 1, 1)
                        dve_psq(dve, piece, piece + 1)
                cast_slot(s, s % RING, s // RING, False)
                for piece in (0, 1):
                    if s == FIRST_SLOT[piece + 1] + 6:
                        dve_hidden1(dve, piece, piece + 1)
                    if s == FIRST_SLOT[piece + 1] + 7:
                        dve_hidden2(dve, piece, piece + 1)
            dve.wait_ge(low_checked, SLOTS)
            nc.vector.reduce_sum(low_sum[:, :], low_sums[:, :], AXIS_X).then_inc(low_sum_ready, 1)
            dve.wait_ge(flag_sum_ready, 1)
            nc.vector.tensor_scalar(flag[:, :], FLAG_BANK[0:1, 0:1], 1.0, None, ALU.min).then_inc(flag_ready, 1)
            dve_psq(dve, 2, 3)
            dve_mix(dve, 2, 3, 0)
            dve_mix(dve, 2, 3, 1)
            dve_hidden1(dve, 2, 3)
            dve_hidden2(dve, 2, 3)

            dve.wait_ge(flag_ready, 1)
            general = dve.value_load(flag[0:1, 0:1], min_val=0, max_val=1)
            with dve.If(general == 1):
                for piece in range(len(PIECES)):
                    t = len(PIECES) + piece + 1
                    dve.wait_ge(y_ready, t - 1)
                    used = [accumulators(0, 0)[0], accumulators(0, 0)[1], accumulators(0, 1)[0],
                            accumulators(0, 1)[1]] if piece == 0 else [
                                bank[(4, 0)[piece - 1] + m][:, :] for m in range(MT)]
                    for b in used + [PSQ_BANK[piece][:, :]]:
                        nc.vector.memset(b, 0.0).then_inc(g_zeroed, 1)
                    with dve.Fori(0, NCH) as c:
                        dve.wait_ge(g_chunk_done, c + (NCH * piece + 1))
                        nc.vector.tensor_copy(psq_slow[:, :], con[:, bass.ds(c * KC + C_WP, KC)]).then_inc(g_psq_w_ready, 1)
                    dve_psq(dve, piece, t)
                    dve_mix(dve, piece, t, 0)
                    dve_mix(dve, piece, t, 1)
                    dve_hidden1(dve, piece, t)
                    dve_hidden2(dve, piece, t)

        @block.tensor
        def _(pe):
            def psq_products(piece, c, j, which, s):
                n, _, per = PIECES[piece]
                pe.wait_ge(x_landed[j], 16 * (s // RING) + 16)
                high = x_raw[:, j].bitcast(BF16).rearrange("p k (n h) -> p k n h", h=2)[:, :, :, 1]
                for kk in range(KC):
                    k = c * KC + kk
                    q = k % PSQ_TILES
                    for part in range(COLS // n):
                        begin = k < PSQ_TILES and which + part == 0
                        end = k >= NK - PSQ_TILES and which == per - 1 and part == COLS // n - 1
                        last = nc.tensor.matmul(PSQ_BANK[piece][PSQ_M * q:PSQ_M * (q + 1), 0:n],
                                                psq_w[:, k, :], high[:, kk, part * n:(part + 1) * n],
                                                start=begin, stop=end, skip_group_check=True)
                last.then_inc(psq_taken, 1)

            def slot(piece, c, which):
                _, _, per = PIECES[piece]
                s = FIRST_SLOT[piece] + c * per + which
                j = s % RING
                psq_products(piece, c, j, which, s)
                if piece == 0 and which == 0:
                    pe.wait_ge(lo_ready, c + 1)
                pe.wait_ge(cast_ready, s + 1)
                for m in range(MT):
                    if piece == 0:
                        target = bank[2 * m + which]
                    else:
                        target = bank[(4, 0)[piece - 1] + m]
                    for kk in range(KC):
                        for part, w_part in enumerate((w_hi, w_lo)):
                            last = nc.tensor.matmul(target[:, :], w_part[:, c * KC + kk, m * P:(m + 1) * P],
                                                    x_cast[:, j, kk, :],
                                                    start=(c + kk + part == 0),
                                                    stop=(c == NCH - 1 and kk == KC - 1 and part == 1))
                    if c == NCH - 1 and which == per - 1 and m < MT - 1:
                        last.then_inc(acc_ready[m], 1)
                last.then_inc(main_done, 1)
                if c == NCH - 1 and which == per - 1:
                    pe.wait_ge(main_done, s + 1)
                    pe.sem_inc(acc_ready[MT - 1], 1)
                    pe.sem_inc(psq_acc_ready, 1)

            pe.wait_ge(psq_w_ready, 2)
            for c in range(NCH):
                for which in range(2):
                    slot(0, c, which)
            pe.wait_ge(ones_set, 3)
            for piece in (1, 2):
                if piece == 2:
                    pe.wait_ge(hidden0_ready, 2 * MT)
                    pe.wait_ge(psq_ready, 1)
                for c in range(NCH):
                    slot(piece, c, 0)
                    if c == 2:
                        pe_l1(pe, piece - 1, piece)
                    if c == 3:
                        pe_l2(pe, piece - 1, piece)
                    if c == 4:
                        pe_l3(pe, piece - 1, piece)
            pe.wait_ge(low_sum_ready, 1)
            nc.tensor.matmul(FLAG_BANK[0:1, 0:1], low_sum[:, :], ones[:, 0:1],
                             start=True, stop=True).then_inc(flag_sum_ready, 1)
            pe_l1(pe, 2, 3)
            pe_l2(pe, 2, 3)
            pe_l3(pe, 2, 3)

            pe.wait_ge(flag_ready, 1)
            general = pe.value_load(flag[0:1, 0:1], min_val=0, max_val=1)
            with pe.If(general == 1):
                pe.sem_inc(g_chunk_done, 1)
                banks_zeroed, loads = 0, 0
                for piece, (n, _, per) in enumerate(PIECES):
                    t = len(PIECES) + piece + 1
                    banks_zeroed += per * MT + 1
                    pe.wait_ge(g_zeroed, banks_zeroed)
                    with pe.Fori(0, NCH) as c:
                        pe.wait_ge(g_landed, c * (16 * (per + 1)) + (loads + 16 * (per + 1)))
                        pe.wait_ge(g_psq_w_ready, c + (NCH * piece + 1))
                        for which in range(per):
                            for kk in range(KC):
                                for m in range(MT):
                                    target = bank[2 * m + which] if piece == 0 else bank[(4, 0)[piece - 1] + m]
                                    nc.tensor.matmul(target[:, :], w_raw[:, 0, kk, m * P:(m + 1) * P],
                                                     x_raw[:, which, kk, :], start=False, stop=False,
                                                     skip_group_check=True)
                                for part in range(COLS // n):
                                    last = nc.tensor.matmul(PSQ_BANK[piece][0:1, 0:n], psq_slow[:, kk:kk + 1],
                                                            x_raw[:, which, kk, part * n:(part + 1) * n],
                                                            start=False, stop=False, skip_group_check=True)
                        last.then_inc(g_chunk_done, 1)
                    loads += 16 * (per + 1) * NCH
                    pe.wait_ge(g_chunk_done, NCH * (piece + 1) + 1)
                    for ready in acc_ready + [psq_acc_ready]:
                        pe.sem_inc(ready, 1)
                    pe_l1(pe, piece, t)
                    pe_l2(pe, piece, t)
                    pe_l3(pe, piece, t)


def kernel(r_wfts, r_bfts, r_stm, L0_rec_ft_w, L0_rec_ft_b, L0_rec_l1_w, L0_rec_l1_b, L0_rec_l2_w,
           L0_rec_l2_b, L0_rec_l3_w, L0_rec_l3_b):
    import numpy as np
    import concourse.bacc as bacc
    from concourse.bass_utils import run_bass_kernel_spmd

    def feature_blocks(a):
        a = np.asarray(a)
        return a.reshape(a.shape[0], NCH, KC, P).transpose(1, 3, 2, 0)

    white, black = feature_blocks(r_wfts), feature_blocks(r_bfts)
    x = np.empty((SLOTS, P, KC, COLS), np.float32)
    for (n, row, per), s in zip(PIECES, FIRST_SLOT):
        if per == 2:
            x[s:s + 2 * NCH:2] = white[..., row:row + n]
            x[s + 1:s + 2 * NCH:2] = black[..., row:row + n]
        else:
            x[s:s + NCH, :, :, 0:n] = white[..., row:row + n]
            x[s:s + NCH, :, :, n:2 * n] = black[..., row:row + n]
    ft_w = np.asarray(L0_rec_ft_w)
    w = np.ascontiguousarray(feature_blocks(ft_w[0:HALF]))
    consts = np.zeros((P, C_ALL), np.float32)
    consts[:, C_FTB:C_FTB + MT] = np.asarray(L0_rec_ft_b)[0:HALF].reshape(MT, P).T
    consts[:, C_W1:C_B1] = np.asarray(L0_rec_l1_w).T.reshape(2 * MT, P, HID).transpose(1, 0, 2).reshape(P, -1)
    consts[0, C_B1:C_W2] = np.asarray(L0_rec_l1_b)
    consts[0:HID, C_W2:C_W3] = np.asarray(L0_rec_l2_w).T
    consts[HID, C_W2:C_W3] = np.asarray(L0_rec_l2_b)
    consts[0:HID, C_W3] = np.asarray(L0_rec_l3_w)[0]
    consts[HID, C_W3] = np.asarray(L0_rec_l3_b)[0]
    consts[0, C_BP] = np.asarray(L0_rec_ft_b)[HALF]
    consts[:, C_WP:C_ALL] = ft_w[HALF].reshape(NK, P).T

    nc = bacc.Bacc("TRN2", target_bir_lowering=False, num_devices=1)
    arrays = {"x": x, "w": w, "consts": consts, "stm": np.ascontiguousarray(np.asarray(r_stm).reshape(BATCH))}
    args = [nc.dram_tensor(name, a.shape, F32, kind="ExternalInput").ap() for name, a in arrays.items()]
    out = nc.dram_tensor("out", (BATCH, 1), F32, kind="ExternalOutput").ap()
    build(nc, *args, out)
    return run_bass_kernel_spmd(nc, [arrays], core_ids=[0]).results[0]["out"]
```

```python
from contextlib import ExitStack

import concourse.bass as bass
from concourse import mybir

F32 = mybir.dt.float32
F32R = mybir.dt.float32r
BF16 = mybir.dt.bfloat16
U16 = mybir.dt.uint16
U8 = mybir.dt.uint8
I32 = mybir.dt.int32
ALU = mybir.AluOpType
ACT = mybir.ActivationFunctionType
AXIS_X = mybir.AxisListType.X

P = 128
BATCH = 1024
FEATURES = 5120
HALF = 256
MT = HALF // P
HID = 32
KC = 4
NCH = FEATURES // (P * KC)
NK = KC * NCH
COLS = 512
PSQ_TILES = 4
PSQ_M = 32
BLOCKS = P // HID
SPREAD = 3

PIECES = [(512, 0, 2), (256, 512, 1), (256, 768, 1)]
FIRST_SLOT = [0, 2 * NCH, 3 * NCH]
END_SLOT = [2 * NCH, 3 * NCH, 4 * NCH]
SLOTS = 4 * NCH
RING = 4
W_RING = 2
FIRST_PARTS = (slice(0, 1), slice(1, 2), slice(2, KC))

C_FTB = 0
C_W1 = C_FTB + MT
C_B1 = C_W1 + 2 * MT * HID
C_W2 = C_B1 + P
C_B2 = C_W2 + P
C_W3 = C_B2 + P
C_B3 = C_W3 + BLOCKS
C_BP = C_B3 + BLOCKS
C_WP = C_BP + 1
C_ALL = C_WP + NK


def build(nc, x, w, consts, stm, out):
    with ExitStack() as ctx:
        def sb(name, shape, dt):
            return ctx.enter_context(nc.sbuf_tensor(name, shape, dt))

        def sem(name):
            return ctx.enter_context(nc.semaphore(name))

        w_hi = sb("w_hi", [P, NK, HALF], F32R)
        w_lo = sb("w_lo", [P, NK, HALF], F32R)
        w_raw = sb("w_raw", [P, W_RING, KC, HALF], F32)
        x_raw = sb("x_raw", [P, RING, KC, COLS], F32)
        x_cast = sb("x_cast", [P, RING, KC, COLS], F32R)
        low_bits = sb("low_bits", [P, 2, KC, COLS], U8)
        low_sums = sb("low_sums", [P, SLOTS], F32)
        low_sum = sb("low_sum", [P, 1], F32)
        flag = sb("flag", [1, 1], I32)
        con = sb("con", [P, C_ALL], F32)
        psq_w = sb("psq_w", [P, NK, PSQ_M], BF16)
        psq_rest = sb("psq_rest", [P, 2, NK], F32)
        psq_bias = sb("psq_bias", [P, 1], F32)
        psq_slow = sb("psq_slow", [P, KC], F32)
        ones = sb("ones", [P, P], F32)
        pick = sb("pick", [P, 2 * BLOCKS - 1], F32)
        side = sb("side", [P, BATCH], F32)
        black = sb("black", [P, MT, COLS], F32)
        diff = sb("diff", [P, COLS], F32)
        moved = sb("moved", [P, COLS], F32)
        hidden0 = sb("hidden0", [P, 2 * MT, COLS], F32)
        psq = sb("psq", [P, COLS], F32)
        side_half = sb("side_half", [P, COLS], F32)
        hidden1 = sb("hidden1", [P, P], F32)
        hidden2 = sb("hidden2", [P, P], F32)
        y = sb("y", [BLOCKS, P], F32)
        bank = [ctx.enter_context(nc.psum_tensor(f"bank{i}", [P, COLS], F32)) for i in range(8)]

        L1_BANK, L2_BANK, FLAG_BANK = bank[2], bank[3], bank[5]
        PSQ_BANK = [bank[6], bank[7], bank[6]]
        Y_BANK = PSQ_BANK
        PSQ_READY = [1, 3, 5, 6, 8, 10]

        def accumulators(piece, m):
            if piece == 0:
                return bank[2 * m][:, :], bank[2 * m + 1][:, :]
            n = PIECES[piece][0]
            b = bank[(4, 0)[piece - 1] + m]
            return b[:, 0:n], b[:, n:2 * n]

        con_landed = sem("con_landed")
        side_landed = sem("side_landed")
        x_first_landed = [sem(f"x_first_landed{i}") for i in range(len(FIRST_PARTS))]
        w_first_landed = [sem(f"w_first_landed{i}") for i in range(len(FIRST_PARTS))]
        hi_first_ready = sem("hi_first_ready")
        lo_first_ready = sem("lo_first_ready")
        cast_first_ready = sem("cast_first_ready")
        x_landed = [sem(f"x_landed{j}") for j in range(RING)]
        w_landed = [sem(f"w_landed{j}") for j in range(W_RING)]
        ones_set = sem("ones_set")
        setup_step = sem("setup_step")
        psq_w_ready = sem("psq_w_ready")
        side_ready = sem("side_ready")
        hi_ready = sem("hi_ready")
        lo_ready = sem("lo_ready")
        cast_ready = sem("cast_ready")
        low_checked = sem("low_checked")
        psq_taken = sem("psq_taken")
        main_done = sem("main_done")
        first_tile_done = sem("first_tile_done")
        g_piece_done = sem("g_piece_done")
        black_ready = sem("black_ready")
        mix_step = sem("mix_step")
        hidden0_ready = sem("hidden0_ready")
        psq_ready = sem("psq_ready")
        l1_done = sem("l1_done")
        hidden1_ready = sem("hidden1_ready")
        l2_done = sem("l2_done")
        hidden2_ready = sem("hidden2_ready")
        y_done = sem("y_done")
        y_ready = sem("y_ready")
        out_landed = sem("out_landed")
        low_sum_ready = sem("low_sum_ready")
        flag_sum_ready = sem("flag_sum_ready")
        flag_ready = sem("flag_ready")
        g_landed = sem("g_landed")
        g_zeroed = sem("g_zeroed")
        g_psq_w_ready = sem("g_psq_w_ready")
        g_chunk_done = sem("g_chunk_done")

        def wait_slot(eng, s, j, i):
            if isinstance(s, int) and s == 0:
                for landed in x_first_landed:
                    eng.wait_ge(landed, 16)
            else:
                eng.wait_ge(x_landed[j], i * 16 + (16 if j > 0 else 0))


        def wait_accumulators(eng, piece, t, m):
            if t > len(PIECES):
                eng.wait_ge(g_piece_done, t - len(PIECES))
            elif m == 0:
                eng.wait_ge(first_tile_done, t)
            else:
                eng.wait_ge(main_done, END_SLOT[piece])

        def act_black(act, piece, t):
            n = PIECES[piece][0]
            for m in range(MT):
                wait_accumulators(act, piece, t, m)
                if t > 1:
                    act.wait_ge(hidden0_ready, 2 * MT * (t - 1))
                nc.scalar.activation(black[:, m, 0:n], accumulators(piece, m)[1], ACT.Identity,
                                     bias=con[:, C_FTB + m:C_FTB + m + 1]).then_inc(black_ready, 1)

        def act_output(act, piece, t):
            n, row, _ = PIECES[piece]
            act.wait_ge(y_done, t)
            if t > 1:
                act.wait_ge(out_landed, 16 * (t - 1))
            nc.scalar.copy(y[:, 0:n // BLOCKS], Y_BANK[piece][0:BLOCKS, 0:n // BLOCKS]).then_inc(y_ready, 1)
            act.wait_ge(y_ready, t)
            act.dma_start(out[row:row + n].rearrange("(q c) a -> q (c a)", q=BLOCKS),
                          y[:, 0:n // BLOCKS]).then_inc(out_landed, 16)

        def dve_mix(dve, piece, t, m):
            n, row, _ = PIECES[piece]
            white = accumulators(piece, m)[0]
            bias = con[:, C_FTB + m:C_FTB + m + 1]
            step = 4 * (MT * (t - 1) + m)
            wait_accumulators(dve, piece, t, m)
            dve.wait_ge(black_ready, MT * (t - 1) + m + 1)
            nc.vector.scalar_tensor_tensor(diff[:, 0:n], white, bias, black[:, m, 0:n],
                                           ALU.add, ALU.subtract).then_inc(mix_step, 1)
            dve.wait_ge(mix_step, step + 1)
            if t == 1:
                dve.wait_ge(side_landed, 16)
            nc.vector.tensor_tensor(moved[:, 0:n], diff[:, 0:n], side[:, row:row + n],
                                    ALU.mult).then_inc(mix_step, 1)
            dve.wait_ge(mix_step, step + 2)
            if t > 1:
                dve.wait_ge(l1_done, t - 1)
            nc.vector.tensor_tensor(hidden0[:, m, 0:n], black[:, m, 0:n], moved[:, 0:n],
                                    ALU.add).then_inc(mix_step, 1)
            nc.vector.scalar_tensor_tensor(hidden0[:, MT + m, 0:n], white, bias, moved[:, 0:n],
                                           ALU.add, ALU.subtract).then_inc(mix_step, 1)
            dve.wait_ge(mix_step, step + 3)
            nc.vector.tensor_scalar(hidden0[:, m, 0:n], hidden0[:, m, 0:n], 0.0, 1.0,
                                    ALU.max, ALU.min).then_inc(hidden0_ready, 1)
            dve.wait_ge(mix_step, step + 4)
            nc.vector.tensor_scalar(hidden0[:, MT + m, 0:n], hidden0[:, MT + m, 0:n], 0.0, 1.0,
                                    ALU.max, ALU.min).then_inc(hidden0_ready, 1)
        def dve_psq(dve, piece, t):
            n, row, _ = PIECES[piece]
            if t > len(PIECES):
                dve.wait_ge(g_piece_done, t - len(PIECES))
            else:
                dve.wait_ge(psq_taken, END_SLOT[piece])
            if t == 1:
                dve.wait_ge(side_landed, 16)
            if t > 1:
                dve.wait_ge(y_done, t - 1)
            nc.vector.tensor_scalar(side_half[:, 0:n], side[:, row:row + n], 0.5, None,
                                    ALU.subtract).then_inc(side_ready, 1)
            dve.wait_ge(side_ready, t)
            for i in range(COLS // n):
                nc.vector.scalar_tensor_tensor(psq[:, i * n:(i + 1) * n], PSQ_BANK[piece][:, i * n:(i + 1) * n],
                                               psq_bias[:, 0:1] if n == COLS else con[:, C_BP:C_BP + 1],
                                               side_half[:, 0:n], ALU.add, ALU.mult).then_inc(psq_ready, 1)

        def dve_hidden1(dve, piece, t):
            n = PIECES[piece][0] // BLOCKS
            dve.wait_ge(l1_done, t)
            nc.vector.tensor_scalar(hidden1[:, 0:n], L1_BANK[:, 0:n], 0.0, 1.0,
                                    ALU.max, ALU.min).then_inc(hidden1_ready, 1)

        def dve_hidden2(dve, piece, t):
            n = PIECES[piece][0] // BLOCKS
            dve.wait_ge(l2_done, t)
            nc.vector.tensor_scalar(hidden2[:, 0:n], L2_BANK[:, 0:n], 0.0, 1.0,
                                    ALU.max, ALU.min).then_inc(hidden2_ready, 1)

        def pe_l1(pe, piece, t):
            n = PIECES[piece][0] // BLOCKS
            if t > 1:
                pe.wait_ge(y_ready, t - 1)
            if piece == 0:
                pe.wait_ge(hidden0_ready, 2 * MT * t)
            pe_psq(pe, piece, t)
            nc.tensor.matmul(L1_BANK[:, 0:n], con[0:1, C_B1:C_B1 + P], ones[0:1, 0:n],
                             start=True, stop=False, skip_group_check=True)
            for m in range(MT):
                pe.wait_ge(hidden0_ready, 2 * (MT * (t - 1) + m + 1))
                for i in (m, MT + m):
                    for q in range(BLOCKS):
                        last = nc.tensor.matmul(L1_BANK[HID * q:HID * (q + 1), 0:n],
                                                con[:, C_W1 + i * HID:C_W1 + (i + 1) * HID],
                                                hidden0[:, i, q * n:(q + 1) * n], start=False,
                                                stop=(i == 2 * MT - 1), skip_group_check=True)
            last.then_inc(l1_done, 1)

        def pe_l2(pe, piece, t):
            n = PIECES[piece][0] // BLOCKS
            nc.tensor.matmul(L2_BANK[:, 0:n], con[0:1, C_B2:C_B2 + P], ones[0:1, 0:n], start=True, stop=False)
            pe.wait_ge(hidden1_ready, t)
            nc.tensor.matmul(L2_BANK[:, 0:n], con[:, C_W2:C_W2 + P], hidden1[:, 0:n],
                             start=False, stop=True).then_inc(l2_done, 1)

        def pe_psq(pe, piece, t):
            n = PIECES[piece][0]
            nb = n // BLOCKS
            rows = Y_BANK[piece][0:BLOCKS, 0:nb]
            pe.wait_ge(psq_ready, PSQ_READY[t - 1])
            if t > 1:
                pe.wait_ge(y_ready, t - 1)
            nc.tensor.matmul(rows, con[0:1, C_B3:C_B3 + BLOCKS], ones[0:1, 0:nb], start=True, stop=False,
                             skip_group_check=True)
            for i in range(COLS // n):
                for q in range(BLOCKS):
                    nc.tensor.matmul(rows, pick[:, BLOCKS - 1 - q:2 * BLOCKS - 1 - q],
                                     psq[:, i * n + q * nb:i * n + (q + 1) * nb], start=False, stop=False,
                                     skip_group_check=True)

        def pe_l3(pe, piece, t):
            nb = PIECES[piece][0] // BLOCKS
            pe.wait_ge(hidden2_ready, t)
            nc.tensor.matmul(Y_BANK[piece][0:BLOCKS, 0:nb], con[:, C_W3:C_W3 + BLOCKS], hidden2[:, 0:nb],
                             start=False, stop=True, skip_group_check=True).then_inc(y_done, 1)

        block = ctx.enter_context(nc.Block())

        @block.sync
        def _(sp):
            def load_weights(c, j, first):
                if not first:
                    sp.wait_ge(lo_ready, c - W_RING + 1)
                sp.dma_start(w_raw[:, j], w[c]).then_inc(w_landed[j], 16)

            def load_slot(s, j, first):
                if not first:
                    sp.wait_ge(psq_taken, s - RING + 1)
                    sp.wait_ge(cast_ready, s - RING + 1)
                    sp.wait_ge(low_checked, s - RING + 1)
                sp.dma_start(x_raw[:, j], x[s]).then_inc(x_landed[j], 16)

            for part, blocks in enumerate(FIRST_PARTS):
                sp.dma_start(w_raw[:, 0, blocks], w[0][:, blocks]).then_inc(w_first_landed[part], 16)
                sp.dma_start(x_raw[:, 0, blocks], x[0][:, blocks]).then_inc(x_first_landed[part], 16)
            sp.dma_start(con[:, :], consts).then_inc(con_landed, 16)
            for j in range(1, RING):
                if j % 2 == 0:
                    load_weights(j // 2, j // 2, True)
                load_slot(j, j, True)
            sp.dma_start(side[:, :], stm.partition_broadcast(P)).then_inc(side_landed, 16)
            with sp.Fori(1, 2 * NCH // RING) as i:
                for j in range(RING):
                    if j % 2 == 0:
                        load_weights(i * W_RING + j // 2, j // 2, False)
                    load_slot(i * RING + j, j, False)
            with sp.Fori(2 * NCH // RING, SLOTS // RING) as i:
                for j in range(RING):
                    load_slot(i * RING + j, j, False)

            sp.wait_ge(flag_ready, 1)
            general = sp.value_load(flag[0:1, 0:1], min_val=0, max_val=1)
            sp.wait_ge(out_landed, 16 * len(PIECES))
            with sp.If(general == 1):
                sp.wait_ge(psq_taken, SLOTS)
                sp.wait_ge(cast_ready, SLOTS)
                sp.wait_ge(low_checked, SLOTS)
                sp.wait_ge(lo_ready, NCH)
                for piece, (_, _, per) in enumerate(PIECES):
                    with sp.Fori(0, NCH) as c:
                        sp.wait_ge(g_chunk_done, c + (NCH * piece + 1))
                        sp.dma_start(w_raw[:, 0], w[c]).then_inc(g_landed, 16)
                        for j in range(per):
                            sp.dma_start(x_raw[:, j], x[c * per + (FIRST_SLOT[piece] + j)]).then_inc(g_landed, 16)
                sp.wait_ge(out_landed, 2 * 16 * len(PIECES))

        @block.gpsimd
        def _(pool):
            nc.gpsimd.memset(ones[:, :], 1.0).then_inc(ones_set, 1)
            nc.gpsimd.memset(pick[:, :], 0.0).then_inc(ones_set, 1)
            pool.wait_ge(ones_set, 2)
            nc.gpsimd.memset(pick[:, BLOCKS - 1:BLOCKS], 1.0).then_inc(ones_set, 1)

        @block.scalar
        def _(act):
            def hi_part(c, j, i):
                act.wait_ge(w_landed[j], i * 16 + (16 if j > 0 else 0))
                nc.scalar.copy(w_hi[:, bass.ds(c * KC, KC), :], w_raw[:, j]).then_inc(hi_ready, 1)

            def check_low_bits(s, j, i, first):
                wait_slot(act, s, j, i)
                if not first:
                    act.wait_ge(low_checked, s - 1)
                bits = x_raw[:, j].bitcast(U16).rearrange("p k (n h) -> p k n h", h=2)[:, :, :, 0]
                nc.scalar.activation(low_bits[:, j % 2], bits, ACT.Copy,
                                     accum_out=low_sums[:, bass.ds(s, 1)]).then_inc(low_checked, 1)

            for part, blocks in enumerate(FIRST_PARTS):
                act.wait_ge(w_first_landed[part], 16)
                nc.scalar.copy(w_hi[:, blocks], w_raw[:, 0, blocks]).then_inc(hi_first_ready, 1)
            for j in range(RING):
                if j == 2:
                    hi_part(1, 1, 0)
                check_low_bits(j, j, 0, j < 2)
            with act.Fori(1, 2 * NCH // RING) as i:
                for j in range(RING):
                    if j % 2 == 0:
                        hi_part(i * W_RING + j // 2, j // 2, i)
                    check_low_bits(i * RING + j, j, i, False)
            for s in range(2 * NCH, SLOTS):
                for piece in (0, 1):
                    if s == FIRST_SLOT[piece + 1] + 3:
                        act_black(act, piece, piece + 1)
                    if s == FIRST_SLOT[piece + 1] + 7:
                        act_output(act, piece, piece + 1)
                check_low_bits(s, s % RING, s // RING, False)
            act_black(act, 2, 3)
            act_output(act, 2, 3)

            act.wait_ge(flag_ready, 1)
            general = act.value_load(flag[0:1, 0:1], min_val=0, max_val=1)
            with act.If(general == 1):
                for piece in range(len(PIECES)):
                    act_black(act, piece, len(PIECES) + piece + 1)
                    act_output(act, piece, len(PIECES) + piece + 1)

        @block.vector
        def _(dve):
            def lo_part(c, j):
                dve.wait_ge(hi_ready, c)
                nc.vector.tensor_tensor(w_lo[:, bass.ds(c * KC, KC), :], w_raw[:, j],
                                        w_hi[:, bass.ds(c * KC, KC), :].bitcast(F32),
                                        ALU.subtract).then_inc(lo_ready, 1)

            def cast_slot(s, j, i, first):
                wait_slot(dve, s, j, i)
                if not first:
                    dve.wait_ge(main_done, s - RING + 1)
                nc.vector.tensor_copy(x_cast[:, j], x_raw[:, j]).then_inc(cast_ready, 1)

            nc.vector.memset(psq_w[:, :, :], 0.0).then_inc(setup_step, 1)
            for part, blocks in enumerate(FIRST_PARTS):
                dve.wait_ge(x_first_landed[part], 16)
                cast = nc.vector.tensor_copy(x_cast[:, 0, blocks], x_raw[:, 0, blocks])
                cast.then_inc(cast_ready if blocks.stop == KC else cast_first_ready, 1)
                dve.wait_ge(hi_first_ready, part + 1)
                low = nc.vector.tensor_tensor(w_lo[:, blocks], w_raw[:, 0, blocks], w_hi[:, blocks].bitcast(F32),
                                              ALU.subtract)
                low.then_inc(lo_ready if blocks.stop == KC else lo_first_ready, 1)
            dve.wait_ge(con_landed, 16)
            nc.vector.tensor_scalar(psq_bias[:, :], con[:, C_BP:C_BP + 1], 2.0, None,
                                    ALU.mult).then_inc(psq_w_ready, 1)
            wp = con[:, C_WP:C_WP + NK]
            dve.wait_ge(setup_step, 1)
            nc.vector.tensor_copy(psq_w[:, :, 0], wp).then_inc(setup_step, 1)
            dve.wait_ge(setup_step, 2)
            nc.vector.tensor_tensor(psq_rest[:, 0, :], wp, psq_w[:, :, 0], ALU.subtract).then_inc(setup_step, 1)
            dve.wait_ge(setup_step, 3)
            nc.vector.tensor_copy(psq_w[:, :, 1], psq_rest[:, 0, :]).then_inc(setup_step, 1)
            dve.wait_ge(setup_step, 4)
            nc.vector.tensor_tensor(psq_rest[:, 1, :], psq_rest[:, 0, :], psq_w[:, :, 1],
                                    ALU.subtract).then_inc(setup_step, 1)
            dve.wait_ge(setup_step, 5)
            nc.vector.tensor_copy(psq_w[:, :, 2], psq_rest[:, 1, :]).then_inc(psq_w_ready, 1)

            for j in range(1, RING):
                if j == 2:
                    lo_part(1, 1)
                cast_slot(j, j, 0, True)
            with dve.Fori(1, 2 * NCH // RING) as i:
                for j in range(RING):
                    if j % 2 == 0:
                        lo_part(i * W_RING + j // 2, j // 2)
                    cast_slot(i * RING + j, j, i, False)
            for s in range(2 * NCH, SLOTS):
                for piece in (0, 1):
                    if s == FIRST_SLOT[piece + 1] + 3:
                        dve_mix(dve, piece, piece + 1, 0)
                    if s == FIRST_SLOT[piece + 1] + 4:
                        dve_mix(dve, piece, piece + 1, 1)
                        dve_psq(dve, piece, piece + 1)
                cast_slot(s, s % RING, s // RING, False)
                for piece in (0, 1):
                    if s == FIRST_SLOT[piece + 1] + 6:
                        dve_hidden1(dve, piece, piece + 1)
                    if s == FIRST_SLOT[piece + 1] + 7:
                        dve_hidden2(dve, piece, piece + 1)
            dve.wait_ge(low_checked, SLOTS)
            nc.vector.reduce_sum(low_sum[:, :], low_sums[:, :], AXIS_X).then_inc(low_sum_ready, 1)
            dve_psq(dve, 2, 3)
            dve_mix(dve, 2, 3, 0)
            dve_mix(dve, 2, 3, 1)
            dve.wait_ge(flag_sum_ready, 1)
            nc.vector.tensor_scalar(flag[:, :], FLAG_BANK[0:1, 0:1], 1.0, None, ALU.min).then_inc(flag_ready, 1)
            dve_hidden1(dve, 2, 3)
            dve_hidden2(dve, 2, 3)

            dve.wait_ge(flag_ready, 1)
            general = dve.value_load(flag[0:1, 0:1], min_val=0, max_val=1)
            with dve.If(general == 1):
                for piece in range(len(PIECES)):
                    t = len(PIECES) + piece + 1
                    dve.wait_ge(y_ready, t - 1)
                    used = [accumulators(0, 0)[0], accumulators(0, 0)[1], accumulators(0, 1)[0],
                            accumulators(0, 1)[1]] if piece == 0 else [
                                bank[(4, 0)[piece - 1] + m][:, :] for m in range(MT)]
                    for b in used + [PSQ_BANK[piece][:, :]]:
                        nc.vector.memset(b, 0.0).then_inc(g_zeroed, 1)
                    with dve.Fori(0, NCH) as c:
                        dve.wait_ge(g_chunk_done, c + (NCH * piece + 1))
                        nc.vector.tensor_copy(psq_slow[:, :], con[:, bass.ds(c * KC + C_WP, KC)]).then_inc(g_psq_w_ready, 1)
                    dve_psq(dve, piece, t)
                    dve_mix(dve, piece, t, 0)
                    dve_mix(dve, piece, t, 1)
                    dve_hidden1(dve, piece, t)
                    dve_hidden2(dve, piece, t)

        @block.tensor
        def _(pe):
            def psq_products(piece, c, j, which, s):
                per = PIECES[piece][2]
                wait_slot(pe, s, j, s // RING)
                high = x_raw[:, j].bitcast(BF16).rearrange("p k (n h) -> p k n h", h=2)[:, :, :, 1]
                for kk in range(KC):
                    k = c * KC + kk
                    q = k % PSQ_TILES
                    last = nc.tensor.matmul(PSQ_BANK[piece][PSQ_M * q:PSQ_M * (q + 1), :],
                                            psq_w[:, k, :], high[:, kk, :],
                                            start=(k < PSQ_TILES and which == 0),
                                            stop=(k >= NK - PSQ_TILES and which == per - 1))
                last.then_inc(psq_taken, 1)

            def main_products(piece, c, which, m, blocks):
                per = PIECES[piece][2]
                j = (FIRST_SLOT[piece] + c * per + which) % RING
                target = bank[2 * m + which] if piece == 0 else bank[(4, 0)[piece - 1] + m]
                for kk in blocks:
                    for part, w_part in enumerate((w_hi, w_lo)):
                        last = nc.tensor.matmul(target[:, :], w_part[:, c * KC + kk, m * P:(m + 1) * P],
                                                x_cast[:, j, kk, :], start=(c + kk + part == 0),
                                                stop=(c == NCH - 1 and kk == KC - 1 and part == 1))
                return last

            def slot(piece, c, which):
                per = PIECES[piece][2]
                s = FIRST_SLOT[piece] + c * per + which
                psq_products(piece, c, s % RING, which, s)
                if piece == 0 and which == 0:
                    pe.wait_ge(lo_ready, c + 1)
                pe.wait_ge(cast_ready, s + 1)
                for m in range(MT):
                    last = main_products(piece, c, which, m, range(KC))
                    if m == 0 and s == END_SLOT[piece] - 1:
                        last.then_inc(first_tile_done, 1)
                last.then_inc(main_done, 1)

            for part, blocks in enumerate(FIRST_PARTS):
                if blocks.stop == KC:
                    pe.wait_ge(cast_ready, 1)
                    pe.wait_ge(lo_ready, 1)
                else:
                    pe.wait_ge(cast_first_ready, part + 1)
                    pe.wait_ge(lo_first_ready, part + 1)
                for kk in range(blocks.start, blocks.stop):
                    for m in range(MT):
                        last = main_products(0, 0, 0, m, [kk])
            last.then_inc(main_done, 1)
            pe.wait_ge(psq_w_ready, 2)
            psq_products(0, 0, 0, 0, 0)
            slot(0, 0, 1)
            for c in range(1, NCH):
                for which in range(2):
                    slot(0, c, which)
            pe.wait_ge(ones_set, 3)
            for piece in (1, 2):
                if piece == 2:
                    pe.wait_ge(hidden0_ready, 2 * MT)
                    pe.wait_ge(psq_ready, 1)
                    pe.wait_ge(y_ready, 1)
                for c in range(NCH if piece == 1 else NCH - SPREAD):
                    slot(piece, c, 0)
                    if c == 2:
                        pe_l1(pe, piece - 1, piece)
                    if c == 3:
                        pe_l2(pe, piece - 1, piece)
                    if c == 4:
                        pe_l3(pe, piece - 1, piece)
            for c in range(NCH - SPREAD, NCH):
                s = FIRST_SLOT[2] + c
                psq_products(2, c, s % RING, 0, s)
                pe.wait_ge(cast_ready, s + 1)
                last = main_products(2, c, 0, 0, range(KC))
            last.then_inc(first_tile_done, 1)
            pe.wait_ge(low_sum_ready, 1)
            nc.tensor.matmul(FLAG_BANK[0:1, 0:1], low_sum[:, :], ones[:, 0:1],
                             start=True, stop=True).then_inc(flag_sum_ready, 1)
            for c in range(NCH - SPREAD, NCH):
                main_products(2, c, 0, 1, range(KC)).then_inc(main_done, 1)
            pe_l1(pe, 2, 3)
            pe_l2(pe, 2, 3)
            pe_l3(pe, 2, 3)

            pe.wait_ge(flag_ready, 1)
            general = pe.value_load(flag[0:1, 0:1], min_val=0, max_val=1)
            with pe.If(general == 1):
                pe.sem_inc(g_chunk_done, 1)
                banks_zeroed, loads = 0, 0
                for piece, (n, _, per) in enumerate(PIECES):
                    t = len(PIECES) + piece + 1
                    banks_zeroed += per * MT + 1
                    pe.wait_ge(g_zeroed, banks_zeroed)
                    with pe.Fori(0, NCH) as c:
                        pe.wait_ge(g_landed, c * (16 * (per + 1)) + (loads + 16 * (per + 1)))
                        pe.wait_ge(g_psq_w_ready, c + (NCH * piece + 1))
                        for which in range(per):
                            for kk in range(KC):
                                for m in range(MT):
                                    target = bank[2 * m + which] if piece == 0 else bank[(4, 0)[piece - 1] + m]
                                    nc.tensor.matmul(target[:, :], w_raw[:, 0, kk, m * P:(m + 1) * P],
                                                     x_raw[:, which, kk, :], start=False, stop=False,
                                                     skip_group_check=True)
                                last = nc.tensor.matmul(PSQ_BANK[piece][0:1, :], psq_slow[:, kk:kk + 1],
                                                        x_raw[:, which, kk, :], start=False, stop=False,
                                                        skip_group_check=True)
                        last.then_inc(g_chunk_done, 1)
                    loads += 16 * (per + 1) * NCH
                    pe.wait_ge(g_chunk_done, NCH * (piece + 1) + 1)
                    pe.sem_inc(g_piece_done, 1)
                    pe_l1(pe, piece, t)
                    pe_l2(pe, piece, t)
                    pe_l3(pe, piece, t)


def kernel(r_wfts, r_bfts, r_stm, L0_rec_ft_w, L0_rec_ft_b, L0_rec_l1_w, L0_rec_l1_b, L0_rec_l2_w,
           L0_rec_l2_b, L0_rec_l3_w, L0_rec_l3_b):
    import numpy as np
    import concourse.bacc as bacc
    from concourse.bass_utils import run_bass_kernel_spmd

    def feature_blocks(a):
        a = np.asarray(a)
        return a.reshape(a.shape[0], NCH, KC, P).transpose(1, 3, 2, 0)

    white, black = feature_blocks(r_wfts), feature_blocks(r_bfts)
    x = np.empty((SLOTS, P, KC, COLS), np.float32)
    for (n, row, per), s in zip(PIECES, FIRST_SLOT):
        if per == 2:
            x[s:s + 2 * NCH:2] = white[..., row:row + n]
            x[s + 1:s + 2 * NCH:2] = black[..., row:row + n]
        else:
            x[s:s + NCH, :, :, 0:n] = white[..., row:row + n]
            x[s:s + NCH, :, :, n:2 * n] = black[..., row:row + n]
    ft_w = np.asarray(L0_rec_ft_w)
    w = np.ascontiguousarray(feature_blocks(ft_w[0:HALF]))
    consts = np.zeros((P, C_ALL), np.float32)
    consts[:, C_FTB:C_FTB + MT] = np.asarray(L0_rec_ft_b)[0:HALF].reshape(MT, P).T
    consts[:, C_W1:C_B1] = np.asarray(L0_rec_l1_w).T.reshape(2 * MT, P, HID).transpose(1, 0, 2).reshape(P, -1)
    consts[0, C_B1:C_W2] = np.tile(np.asarray(L0_rec_l1_b), BLOCKS)
    for q in range(BLOCKS):
        units = slice(q * HID, (q + 1) * HID)
        consts[units, C_W2 + q * HID:C_W2 + (q + 1) * HID] = np.asarray(L0_rec_l2_w).T
        consts[units, C_W3 + q] = np.asarray(L0_rec_l3_w)[0]
    consts[0, C_B2:C_W3] = np.tile(np.asarray(L0_rec_l2_b), BLOCKS)
    consts[0, C_B3:C_BP] = np.asarray(L0_rec_l3_b)[0]
    consts[0, C_BP] = np.asarray(L0_rec_ft_b)[HALF]
    consts[:, C_WP:C_ALL] = ft_w[HALF].reshape(NK, P).T

    nc = bacc.Bacc("TRN2", target_bir_lowering=False, num_devices=1)
    arrays = {"x": x, "w": w, "consts": consts, "stm": np.ascontiguousarray(np.asarray(r_stm).reshape(BATCH))}
    args = [nc.dram_tensor(name, a.shape, F32, kind="ExternalInput").ap() for name, a in arrays.items()]
    out = nc.dram_tensor("out", (BATCH, 1), F32, kind="ExternalOutput").ap()
    build(nc, *args, out)
    return run_bass_kernel_spmd(nc, [arrays], core_ids=[0]).results[0]["out"]
```

```python
from contextlib import ExitStack

import concourse.bass as bass
from concourse import mybir

F32 = mybir.dt.float32
F32R = mybir.dt.float32r
BF16 = mybir.dt.bfloat16
U16 = mybir.dt.uint16
U8 = mybir.dt.uint8
I32 = mybir.dt.int32
ALU = mybir.AluOpType
ACT = mybir.ActivationFunctionType
AXIS_X = mybir.AxisListType.X

P = 128
BATCH = 1024
FEATURES = 5120
HALF = 256
MT = HALF // P
HID = 32
KC = 4
NCH = FEATURES // (P * KC)
NK = KC * NCH
COLS = 512
PSQ_M = 32
BLOCKS = P // HID
SPREAD = 3

RING = 4
W_RING = 2

PIECES = [(512, 0, 2), (256, 512, 1), (256, 768, 1)]
FIRST_BLOCK = [0, 2 * NCH, 3 * NCH]
ORDER = ([slot for c in range(NCH) for slot in ((0, c, 0), (0, c, 1), (1, c, 0))]
         + [(2, c, 0) for c in range(NCH)])
SLOTS = len(ORDER)
END_SLOT = [max(s for s, slot in enumerate(ORDER) if slot[0] == piece) + 1 for piece in range(len(PIECES))]
LOOP_START = 6
LOOP_CHUNKS = 4
LOOP_SLOTS = 3 * LOOP_CHUNKS
LOOPS = (NCH - 2) // LOOP_CHUNKS
LOOP_END = LOOP_START + LOOPS * LOOP_SLOTS
DVE_PSQ = sorted({s for s in range(1, LOOP_END) if s % LOOP_SLOTS in (1, 2, 4, 6, 8, 10, 11)}
                 | {31, 33, 38, 39})


def psq_count(s):
    return 2 * sum((other in DVE_PSQ) == (s in DVE_PSQ) for other in range(s + 1))


def psq_per_loop(s):
    return 2 * sum((other in DVE_PSQ) == (s in DVE_PSQ) for other in range(LOOP_START, LOOP_START + LOOP_SLOTS))


DVE_PSQ_SUM = (31, 37)
DVE_MIX = ((31, 32), (35, 36))
PE_LAYERS = (31, 36)
DVE_HIDDEN = (35, SLOTS)
ACT_BLACK = (31, 34)
ACT_OUTPUT = (37, SLOTS)
FIRST_PARTS = (slice(0, 1), slice(1, 2), slice(2, KC))

C_FTB = 0
C_W1 = C_FTB + MT
C_B1 = C_W1 + 2 * MT * HID
C_W2 = C_B1 + P
C_B2 = C_W2 + P
C_W3 = C_B2 + P
C_B3 = C_W3 + BLOCKS
C_BP = C_B3 + BLOCKS
C_WP = C_BP + 1
C_ALL = C_WP + NK


def psq_slots(piece, vector):
    return [s for s in range(SLOTS) if ORDER[s][0] == piece and (s in DVE_PSQ) == vector]


LAST_DVE_PSQ = [psq_slots(piece, True)[-1] for piece in range(len(PIECES))]
LAST_PE_PSQ = [psq_slots(piece, False)[-1] for piece in range(len(PIECES))]


def build(nc, x, w, consts, stm, out):
    with ExitStack() as ctx:
        def sb(name, shape, dt):
            return ctx.enter_context(nc.sbuf_tensor(name, shape, dt))

        def sem(name):
            return ctx.enter_context(nc.semaphore(name))

        w_hi = sb("w_hi", [P, NK, HALF], F32R)
        w_lo = sb("w_lo", [P, NK, HALF], F32R)
        w_raw = sb("w_raw", [P, W_RING, KC, HALF], F32)
        x_raw = sb("x_raw", [P, RING, KC, COLS], F32)
        x_cast = sb("x_cast", [P, RING, KC, COLS], F32R)
        low_bits = sb("low_bits", [P, 2, KC, COLS], U8)
        low_sums = sb("low_sums", [P, SLOTS], F32)
        low_sum = sb("low_sum", [P, 1], F32)
        flag = sb("flag", [1, 1], I32)
        con = sb("con", [P, C_ALL], F32)
        psq_w = sb("psq_w", [P, NK, PSQ_M], BF16)
        psq_rest = sb("psq_rest", [P, 2, NK], F32)
        psq_bias = sb("psq_bias", [P, 1], F32)
        psq_slow = sb("psq_slow", [P, KC], F32)
        ones = sb("ones", [P, P], F32)
        pick = sb("pick", [P, 2 * BLOCKS - 1], F32)
        side = sb("side", [P, BATCH], F32)
        black = sb("black", [P, MT, COLS], F32)
        diff = sb("diff", [P, COLS], F32)
        moved = sb("moved", [P, COLS], F32)
        hidden0 = sb("hidden0", [P, 2 * MT, COLS], F32)
        psq_acc = sb("psq_acc", [P, 2, 2, COLS], F32)
        psq = sb("psq", [P, COLS], F32)
        side_half = sb("side_half", [P, COLS], F32)
        hidden1 = sb("hidden1", [P, P], F32)
        hidden2 = sb("hidden2", [P, P], F32)
        y = sb("y", [BLOCKS, P], F32)
        bank = [ctx.enter_context(nc.psum_tensor(f"bank{i}", [P, COLS], F32)) for i in range(8)]

        L1_BANK, L2_BANK, FLAG_BANK = bank[3], bank[3], bank[5]
        PSQ_BANK = [bank[6], bank[7], bank[6]]
        Y_ROWS = bank[2][0:BLOCKS, 0:P]

        def accumulators(piece, m):
            if piece == 0:
                return bank[2 * m][:, :], bank[2 * m + 1][:, :]
            n = PIECES[piece][0]
            b = bank[(4, 0)[piece - 1] + m]
            return b[:, 0:n], b[:, n:2 * n]

        con_landed = sem("con_landed")
        side_landed = sem("side_landed")
        x_first_landed = [sem(f"x_first_landed{i}") for i in range(len(FIRST_PARTS))]
        w_first_landed = [sem(f"w_first_landed{i}") for i in range(len(FIRST_PARTS))]
        hi_first_ready = sem("hi_first_ready")
        lo_first_ready = sem("lo_first_ready")
        cast_first_ready = sem("cast_first_ready")
        x_landed = [sem(f"x_landed{j}") for j in range(RING)]
        w_landed = [sem(f"w_landed{j}") for j in range(W_RING)]
        ones_set = sem("ones_set")
        setup_step = sem("setup_step")
        psq_w_ready = sem("psq_w_ready")
        side_ready = sem("side_ready")
        hi_ready = sem("hi_ready")
        lo_ready = sem("lo_ready")
        cast_ready = sem("cast_ready")
        low_checked = sem("low_checked")
        psq_taken = sem("psq_taken")
        psq_added = sem("psq_added")
        psq_step = sem("psq_step")
        main_done = sem("main_done")
        first_tile_done = sem("first_tile_done")
        g_piece_done = sem("g_piece_done")
        black_ready = sem("black_ready")
        mix_step = sem("mix_step")
        hidden0_ready = sem("hidden0_ready")
        psq_ready = sem("psq_ready")
        l1_done = sem("l1_done")
        hidden1_ready = sem("hidden1_ready")
        l2_done = sem("l2_done")
        hidden2_ready = sem("hidden2_ready")
        y_done = sem("y_done")
        y_ready = sem("y_ready")
        out_landed = sem("out_landed")
        low_sum_ready = sem("low_sum_ready")
        flag_sum_ready = sem("flag_sum_ready")
        flag_ready = sem("flag_ready")
        g_landed = sem("g_landed")
        g_zeroed = sem("g_zeroed")
        g_psq_w_ready = sem("g_psq_w_ready")
        g_chunk_done = sem("g_chunk_done")

        def wait_slot(eng, s, i):
            j = s % RING
            if s == 0:
                for landed in x_first_landed:
                    eng.wait_ge(landed, 16)
            else:
                eng.wait_ge(x_landed[j], i * (16 * LOOP_SLOTS // RING) + 16 * (s // RING + (j > 0)))


        def wait_accumulators(eng, piece, t, m):
            if t > len(PIECES):
                eng.wait_ge(g_piece_done, t - len(PIECES))
            elif m == 0:
                eng.wait_ge(first_tile_done, t)
            else:
                eng.wait_ge(main_done, END_SLOT[piece])

        def act_black(act, piece, t):
            n = PIECES[piece][0]
            for m in range(MT):
                wait_accumulators(act, piece, t, m)
                if t > 1:
                    act.wait_ge(hidden0_ready, 2 * MT * (t - 1))
                nc.scalar.activation(black[:, m, 0:n], accumulators(piece, m)[1], ACT.Identity,
                                     bias=con[:, C_FTB + m:C_FTB + m + 1]).then_inc(black_ready, 1)

        def act_output(act, piece, t):
            n, row, _ = PIECES[piece]
            act.wait_ge(y_done, t)
            if t > 1:
                act.wait_ge(out_landed, 16 * (t - 1))
            nc.scalar.copy(y[:, 0:n // BLOCKS], Y_ROWS[:, 0:n // BLOCKS]).then_inc(y_ready, 1)
            act.wait_ge(y_ready, t)
            act.dma_start(out[row:row + n].rearrange("(q c) a -> q (c a)", q=BLOCKS),
                          y[:, 0:n // BLOCKS]).then_inc(out_landed, 16)

        def dve_mix(dve, piece, t, m):
            n, row, _ = PIECES[piece]
            white = accumulators(piece, m)[0]
            bias = con[:, C_FTB + m:C_FTB + m + 1]
            step = 4 * (MT * (t - 1) + m)
            wait_accumulators(dve, piece, t, m)
            dve.wait_ge(black_ready, MT * (t - 1) + m + 1)
            nc.vector.scalar_tensor_tensor(diff[:, 0:n], white, bias, black[:, m, 0:n],
                                           ALU.add, ALU.subtract).then_inc(mix_step, 1)
            dve.wait_ge(mix_step, step + 1)
            if t == 1:
                dve.wait_ge(side_landed, 16)
            nc.vector.tensor_tensor(moved[:, 0:n], diff[:, 0:n], side[:, row:row + n],
                                    ALU.mult).then_inc(mix_step, 1)
            dve.wait_ge(mix_step, step + 2)
            if t > 1:
                dve.wait_ge(l1_done, t - 1)
            nc.vector.tensor_tensor(hidden0[:, m, 0:n], black[:, m, 0:n], moved[:, 0:n],
                                    ALU.add).then_inc(mix_step, 1)
            nc.vector.scalar_tensor_tensor(hidden0[:, MT + m, 0:n], white, bias, moved[:, 0:n],
                                           ALU.add, ALU.subtract).then_inc(mix_step, 1)
            dve.wait_ge(mix_step, step + 3)
            nc.vector.tensor_scalar(hidden0[:, m, 0:n], hidden0[:, m, 0:n], 0.0, 1.0,
                                    ALU.max, ALU.min).then_inc(hidden0_ready, 1)
            dve.wait_ge(mix_step, step + 4)
            nc.vector.tensor_scalar(hidden0[:, MT + m, 0:n], hidden0[:, MT + m, 0:n], 0.0, 1.0,
                                    ALU.max, ALU.min).then_inc(hidden0_ready, 1)
        def dve_psq(dve, piece, t):
            n, row, _ = PIECES[piece]
            if t > len(PIECES):
                dve.wait_ge(g_piece_done, t - len(PIECES))
            else:
                dve.wait_ge(psq_taken, psq_count(LAST_PE_PSQ[piece]))
            if t == 1:
                dve.wait_ge(side_landed, 16)
            if t > 1:
                dve.wait_ge(y_done, t - 1)
            nc.vector.tensor_scalar(side_half[:, 0:n], side[:, row:row + n], 0.5, None,
                                    ALU.subtract).then_inc(side_ready, 1)
            acc = psq_acc[:, piece % 2]
            if t <= len(PIECES):
                dve.wait_ge(psq_added, psq_count(LAST_DVE_PSQ[piece]))
            step = 3 * (t - 1)
            nc.vector.tensor_tensor(acc[:, 0], acc[:, 0], acc[:, 1], ALU.add).then_inc(psq_step, 1)
            dve.wait_ge(psq_step, step + 1)
            nc.vector.tensor_tensor(acc[:, 0], PSQ_BANK[piece][:, :], acc[:, 0], ALU.add).then_inc(psq_step, 1)
            dve.wait_ge(psq_step, step + 2)
            if n < COLS:
                nc.vector.tensor_tensor(acc[:, 0, 0:n], acc[:, 0, 0:n], acc[:, 0, n:2 * n],
                                        ALU.add).then_inc(psq_step, 1)
            else:
                dve.sem_inc(psq_step, 1)
            dve.wait_ge(psq_step, step + 3)
            dve.wait_ge(side_ready, t)
            nc.vector.scalar_tensor_tensor(psq[:, 0:n], acc[:, 0, 0:n], psq_bias[:, 0:1], side_half[:, 0:n],
                                           ALU.add, ALU.mult).then_inc(psq_ready, 1)

        def dve_hidden1(dve, piece, t):
            n = PIECES[piece][0] // BLOCKS
            dve.wait_ge(l1_done, t)
            nc.vector.tensor_scalar(hidden1[:, 0:n], L1_BANK[:, 0:n], 0.0, 1.0,
                                    ALU.max, ALU.min).then_inc(hidden1_ready, 1)

        def dve_hidden2(dve, piece, t):
            n = PIECES[piece][0] // BLOCKS
            dve.wait_ge(l2_done, t)
            nc.vector.tensor_scalar(hidden2[:, 0:n], L2_BANK[:, 0:n], 0.0, 1.0,
                                    ALU.max, ALU.min).then_inc(hidden2_ready, 1)

        def pe_l1(pe, piece, t):
            n = PIECES[piece][0] // BLOCKS
            if t > 1:
                pe.wait_ge(y_ready, t - 1)
            if piece == 0:
                pe.wait_ge(hidden0_ready, 2 * MT * t)
            pe_psq(pe, piece, t)
            nc.tensor.matmul(L1_BANK[:, 0:n], con[0:1, C_B1:C_B1 + P], ones[0:1, 0:n],
                             start=True, stop=False, skip_group_check=True)
            for m in range(MT):
                pe.wait_ge(hidden0_ready, 2 * (MT * (t - 1) + m + 1))
                for i in (m, MT + m):
                    for q in range(BLOCKS):
                        last = nc.tensor.matmul(L1_BANK[HID * q:HID * (q + 1), 0:n],
                                                con[:, C_W1 + i * HID:C_W1 + (i + 1) * HID],
                                                hidden0[:, i, q * n:(q + 1) * n], start=False,
                                                stop=(i == 2 * MT - 1), skip_group_check=True)
            last.then_inc(l1_done, 1)

        def pe_l2(pe, piece, t):
            n = PIECES[piece][0] // BLOCKS
            pe.wait_ge(hidden1_ready, t)
            nc.tensor.matmul(L2_BANK[:, 0:n], con[0:1, C_B2:C_B2 + P], ones[0:1, 0:n], start=True, stop=False)
            nc.tensor.matmul(L2_BANK[:, 0:n], con[:, C_W2:C_W2 + P], hidden1[:, 0:n],
                             start=False, stop=True).then_inc(l2_done, 1)

        def pe_psq(pe, piece, t):
            n = PIECES[piece][0]
            nb = n // BLOCKS
            rows = Y_ROWS[:, 0:nb]
            pe.wait_ge(psq_ready, t)
            if t > 1:
                pe.wait_ge(y_ready, t - 1)
            nc.tensor.matmul(rows, con[0:1, C_B3:C_B3 + BLOCKS], ones[0:1, 0:nb], start=True, stop=False,
                             skip_group_check=True)
            for q in range(BLOCKS):
                nc.tensor.matmul(rows, pick[:, BLOCKS - 1 - q:2 * BLOCKS - 1 - q], psq[:, q * nb:(q + 1) * nb],
                                 start=False, stop=False, skip_group_check=True)

        def pe_l3(pe, piece, t):
            nb = PIECES[piece][0] // BLOCKS
            pe.wait_ge(hidden2_ready, t)
            nc.tensor.matmul(Y_ROWS[:, 0:nb], con[:, C_W3:C_W3 + BLOCKS], hidden2[:, 0:nb],
                             start=False, stop=True, skip_group_check=True).then_inc(y_done, 1)

        block = ctx.enter_context(nc.Block())

        @block.sync
        def _(sp):
            def load_weights(c, j):
                if not isinstance(c, int) or c >= W_RING:
                    sp.wait_ge(lo_ready, c - W_RING + 1)
                sp.dma_start(w_raw[:, j], w[c]).then_inc(w_landed[j], 16)

            def load_slot(s, i):
                piece, c, which = ORDER[s]
                per = PIECES[piece][2]
                block = i * (LOOP_CHUNKS * per) + (FIRST_BLOCK[piece] + c * per + which)
                if s >= RING:
                    last = s - RING
                    psq_before = i * psq_per_loop(last) + psq_count(last)
                    before = i * LOOP_SLOTS + (last + 1)
                    if not isinstance(i, int):
                        psq_before, before = sp.to_reg(psq_before), sp.to_reg(before)
                    sp.wait_ge(psq_added if last in DVE_PSQ else psq_taken, psq_before)
                    sp.wait_ge(cast_ready, before)
                    sp.wait_ge(low_checked, before)
                sp.dma_start(x_raw[:, s % RING], x[block]).then_inc(x_landed[s % RING], 16)

            for part, blocks in enumerate(FIRST_PARTS):
                sp.dma_start(w_raw[:, 0, blocks], w[0][:, blocks]).then_inc(w_first_landed[part], 16)
                sp.dma_start(x_raw[:, 0, blocks], x[0][:, blocks]).then_inc(x_first_landed[part], 16)
            sp.dma_start(con[:, :], consts).then_inc(con_landed, 16)
            for s in range(1, LOOP_START):
                if s == 3:
                    load_weights(1, 1)
                load_slot(s, 0)
            with sp.Fori(0, LOOPS) as i:
                for s in range(LOOP_START, LOOP_START + LOOP_SLOTS):
                    piece, c, which = ORDER[s]
                    if (piece, which) == (0, 0):
                        load_weights(i * LOOP_CHUNKS + c, c % W_RING)
                    load_slot(s, i)
            sp.dma_start(side[:, :], stm.partition_broadcast(P)).then_inc(side_landed, 16)
            for s in range(LOOP_END, SLOTS):
                load_slot(s, 0)

            sp.wait_ge(flag_ready, 1)
            general = sp.value_load(flag[0:1, 0:1], min_val=0, max_val=1)
            sp.wait_ge(out_landed, 16 * len(PIECES))
            with sp.If(general == 1):
                sp.wait_ge(psq_taken, psq_count(LAST_PE_PSQ[-1]))
                sp.wait_ge(psq_added, psq_count(LAST_DVE_PSQ[-1]))
                sp.wait_ge(cast_ready, SLOTS)
                sp.wait_ge(low_checked, SLOTS)
                sp.wait_ge(lo_ready, NCH)
                for piece, (_, _, per) in enumerate(PIECES):
                    with sp.Fori(0, NCH) as c:
                        sp.wait_ge(g_chunk_done, c + (NCH * piece + 1))
                        sp.dma_start(w_raw[:, 0], w[c]).then_inc(g_landed, 16)
                        for j in range(per):
                            sp.dma_start(x_raw[:, j], x[c * per + (FIRST_BLOCK[piece] + j)]).then_inc(g_landed, 16)
                sp.wait_ge(out_landed, 2 * 16 * len(PIECES))

        @block.gpsimd
        def _(pool):
            nc.gpsimd.memset(ones[:, :], 1.0).then_inc(ones_set, 1)
            nc.gpsimd.memset(pick[:, :], 0.0).then_inc(ones_set, 1)
            pool.wait_ge(ones_set, 2)
            nc.gpsimd.memset(pick[:, BLOCKS - 1:BLOCKS], 1.0).then_inc(ones_set, 1)

        @block.scalar
        def _(act):
            def hi_part(c, i):
                j = c % W_RING
                act.wait_ge(w_landed[j], i * (16 * LOOP_CHUNKS // W_RING) + 16 * (c // W_RING + (j > 0)))
                nc.scalar.copy(w_hi[:, bass.ds(i * (LOOP_CHUNKS * KC) + c * KC, KC), :], w_raw[:, j]).then_inc(hi_ready, 1)

            def check_low_bits(s, i):
                j = s % RING
                wait_slot(act, s, i)
                if s >= 2:
                    act.wait_ge(low_checked, i * LOOP_SLOTS + (s - 1))
                bits = x_raw[:, j].bitcast(U16).rearrange("p k (n h) -> p k n h", h=2)[:, :, :, 0]
                nc.scalar.activation(low_bits[:, j % 2], bits, ACT.Copy,
                                     accum_out=low_sums[:, bass.ds(i * LOOP_SLOTS + s, 1)]).then_inc(low_checked, 1)

            for part, blocks in enumerate(FIRST_PARTS):
                act.wait_ge(w_first_landed[part], 16)
                nc.scalar.copy(w_hi[:, blocks], w_raw[:, 0, blocks]).then_inc(hi_first_ready, 1)
            for s in range(LOOP_START):
                if s == 3:
                    hi_part(1, 0)
                check_low_bits(s, 0)
            with act.Fori(0, LOOPS) as i:
                for s in range(LOOP_START, LOOP_START + LOOP_SLOTS):
                    piece, c, which = ORDER[s]
                    if (piece, which) == (0, 0):
                        hi_part(c, i)
                    check_low_bits(s, i)
            for s in range(LOOP_END, SLOTS):
                for piece in (0, 1):
                    if s == ACT_BLACK[piece]:
                        act_black(act, piece, piece + 1)
                    if s == ACT_OUTPUT[piece]:
                        act_output(act, piece, piece + 1)
                check_low_bits(s, 0)
            act_output(act, 1, 2)
            act_black(act, 2, 3)
            act_output(act, 2, 3)

            act.wait_ge(flag_ready, 1)
            general = act.value_load(flag[0:1, 0:1], min_val=0, max_val=1)
            with act.If(general == 1):
                for piece in range(len(PIECES)):
                    act_black(act, piece, len(PIECES) + piece + 1)
                    act_output(act, piece, len(PIECES) + piece + 1)

        @block.vector
        def _(dve):
            def lo_part(c, j):
                dve.wait_ge(hi_ready, c)
                nc.vector.tensor_tensor(w_lo[:, bass.ds(c * KC, KC), :], w_raw[:, j],
                                        w_hi[:, bass.ds(c * KC, KC), :].bitcast(F32),
                                        ALU.subtract).then_inc(lo_ready, 1)

            def cast_slot(s, i):
                j = s % RING
                wait_slot(dve, s, i)
                if s >= RING:
                    dve.wait_ge(main_done, i * LOOP_SLOTS + (s - RING + 1))
                nc.vector.tensor_copy(x_cast[:, j], x_raw[:, j]).then_inc(cast_ready, 1)

            nc.vector.memset(psq_w[:, :, :], 0.0).then_inc(setup_step, 1)
            for part, blocks in enumerate(FIRST_PARTS):
                dve.wait_ge(x_first_landed[part], 16)
                cast = nc.vector.tensor_copy(x_cast[:, 0, blocks], x_raw[:, 0, blocks])
                cast.then_inc(cast_ready if blocks.stop == KC else cast_first_ready, 1)
                dve.wait_ge(hi_first_ready, part + 1)
                low = nc.vector.tensor_tensor(w_lo[:, blocks], w_raw[:, 0, blocks], w_hi[:, blocks].bitcast(F32),
                                              ALU.subtract)
                low.then_inc(lo_ready if blocks.stop == KC else lo_first_ready, 1)
            dve.wait_ge(con_landed, 16)
            nc.vector.tensor_scalar(psq_bias[:, :], con[:, C_BP:C_BP + 1], 2.0, None,
                                    ALU.mult).then_inc(psq_w_ready, 1)
            wp = con[:, C_WP:C_WP + NK]
            dve.wait_ge(setup_step, 1)
            nc.vector.tensor_copy(psq_w[:, :, 0], wp).then_inc(setup_step, 1)
            dve.wait_ge(setup_step, 2)
            nc.vector.tensor_tensor(psq_rest[:, 0, :], wp, psq_w[:, :, 0], ALU.subtract).then_inc(setup_step, 1)
            dve.wait_ge(setup_step, 3)
            nc.vector.tensor_copy(psq_w[:, :, 1], psq_rest[:, 0, :]).then_inc(setup_step, 1)
            dve.wait_ge(setup_step, 4)
            nc.vector.tensor_tensor(psq_rest[:, 1, :], psq_rest[:, 0, :], psq_w[:, :, 1],
                                    ALU.subtract).then_inc(setup_step, 1)
            dve.wait_ge(setup_step, 5)
            nc.vector.tensor_copy(psq_w[:, :, 2], psq_rest[:, 1, :]).then_inc(psq_w_ready, 1)

            def add_psq(s, i):
                piece, c, _ = ORDER[s]
                j = s % RING
                before = i * psq_per_loop(s) + (psq_count(s) - 2)
                begins = s == psq_slots(piece, True)[0]
                for kk in range(KC):
                    acc = psq_acc[:, piece % 2, kk % 2]
                    weight = con[:, bass.ds(i * (LOOP_CHUNKS * KC) + (C_WP + c * KC + kk), 1)]
                    if kk == 0 and psq_count(s) > 2:
                        dve.wait_ge(psq_added, before)
                    if kk == 2:
                        dve.wait_ge(psq_added, before + 1)
                    if begins and kk < 2:
                        done = nc.vector.tensor_scalar(acc, x_raw[:, j, kk], weight, None, ALU.mult)
                    else:
                        done = nc.vector.scalar_tensor_tensor(acc, x_raw[:, j, kk], weight, acc, ALU.mult, ALU.add)
                    if kk % 2 == 1:
                        done.then_inc(psq_added, 1)

            for s in range(1, LOOP_START):
                if s == 3:
                    lo_part(1, 1)
                cast_slot(s, 0)
                if s in DVE_PSQ:
                    add_psq(s, 0)
            with dve.Fori(0, LOOPS) as i:
                for s in range(LOOP_START, LOOP_START + LOOP_SLOTS):
                    piece, c, which = ORDER[s]
                    if (piece, which) == (0, 0):
                        lo_part(i * LOOP_CHUNKS + c, c % W_RING)
                    cast_slot(s, i)
                    if s in DVE_PSQ:
                        add_psq(s, i)
            for s in range(LOOP_END, SLOTS):
                for piece in (0, 1):
                    if s == DVE_PSQ_SUM[piece]:
                        dve_psq(dve, piece, piece + 1)
                    for m in range(MT):
                        if s == DVE_MIX[piece][m]:
                            dve_mix(dve, piece, piece + 1, m)
                    if s == DVE_HIDDEN[piece]:
                        dve_hidden1(dve, piece, piece + 1)
                    if s == DVE_HIDDEN[piece] + 1:
                        dve_hidden2(dve, piece, piece + 1)
                cast_slot(s, 0)
                if s in DVE_PSQ:
                    add_psq(s, 0)
            dve_hidden1(dve, 1, 2)
            dve_hidden2(dve, 1, 2)
            dve.wait_ge(low_checked, SLOTS)
            nc.vector.reduce_sum(low_sum[:, :], low_sums[:, :], AXIS_X).then_inc(low_sum_ready, 1)
            dve_psq(dve, 2, 3)
            dve_mix(dve, 2, 3, 0)
            dve_mix(dve, 2, 3, 1)
            dve.wait_ge(flag_sum_ready, 1)
            nc.vector.tensor_scalar(flag[:, :], FLAG_BANK[0:1, 0:1], 1.0, None, ALU.min).then_inc(flag_ready, 1)
            dve_hidden1(dve, 2, 3)
            dve_hidden2(dve, 2, 3)

            dve.wait_ge(flag_ready, 1)
            general = dve.value_load(flag[0:1, 0:1], min_val=0, max_val=1)
            with dve.If(general == 1):
                for piece in range(len(PIECES)):
                    t = len(PIECES) + piece + 1
                    dve.wait_ge(y_ready, t - 1)
                    used = [accumulators(0, 0)[0], accumulators(0, 0)[1], accumulators(0, 1)[0],
                            accumulators(0, 1)[1]] if piece == 0 else [
                                bank[(4, 0)[piece - 1] + m][:, :] for m in range(MT)]
                    for b in used + [PSQ_BANK[piece][:, :], psq_acc[:, piece % 2]]:
                        nc.vector.memset(b, 0.0).then_inc(g_zeroed, 1)
                    with dve.Fori(0, NCH) as c:
                        dve.wait_ge(g_chunk_done, c + (NCH * piece + 1))
                        nc.vector.tensor_copy(psq_slow[:, :], con[:, bass.ds(c * KC + C_WP, KC)]).then_inc(g_psq_w_ready, 1)
                    dve_psq(dve, piece, t)
                    dve_mix(dve, piece, t, 0)
                    dve_mix(dve, piece, t, 1)
                    dve_hidden1(dve, piece, t)
                    dve_hidden2(dve, piece, t)

        @block.tensor
        def _(pe):
            def psq_products(s):
                wait_slot(pe, s, 0)
                piece, c, _ = ORDER[s]
                high = x_raw[:, s % RING].bitcast(BF16).rearrange("p k (n h) -> p k n h", h=2)[:, :, :, 1]
                for kk in range(KC):
                    last = nc.tensor.matmul(PSQ_BANK[piece][PSQ_M * kk:PSQ_M * (kk + 1), :],
                                            psq_w[:, c * KC + kk, :], high[:, kk, :], start=(s == psq_slots(piece, False)[0]),
                                            stop=(s == LAST_PE_PSQ[piece]))
                last.then_inc(psq_taken, 2)

            def main_products(s, m, blocks):
                piece, c, which = ORDER[s]
                target = bank[2 * m + which] if piece == 0 else bank[(4, 0)[piece - 1] + m]
                for kk in blocks:
                    for part, w_part in enumerate((w_hi, w_lo)):
                        last = nc.tensor.matmul(target[:, :], w_part[:, c * KC + kk, m * P:(m + 1) * P],
                                                x_cast[:, s % RING, kk, :], start=(c + kk + part == 0),
                                                stop=(c == NCH - 1 and kk == KC - 1 and part == 1))
                return last

            def slot(s):
                piece, c, which = ORDER[s]
                if s not in DVE_PSQ:
                    psq_products(s)
                if (piece, which) == (0, 0):
                    pe.wait_ge(lo_ready, c + 1)
                pe.wait_ge(cast_ready, s + 1)
                for m in range(MT):
                    last = main_products(s, m, range(KC))
                    if m == 0 and s == END_SLOT[piece] - 1:
                        last.then_inc(first_tile_done, 1)
                last.then_inc(main_done, 1)

            def pe_small_layers(s):
                for piece in (0, 1):
                    for step, layer in enumerate((pe_l1, pe_l2, pe_l3)):
                        if s == PE_LAYERS[piece] + step:
                            layer(pe, piece, piece + 1)

            for part, blocks in enumerate(FIRST_PARTS):
                if blocks.stop == KC:
                    pe.wait_ge(cast_ready, 1)
                    pe.wait_ge(lo_ready, 1)
                else:
                    pe.wait_ge(cast_first_ready, part + 1)
                    pe.wait_ge(lo_first_ready, part + 1)
                for kk in range(blocks.start, blocks.stop):
                    for m in range(MT):
                        last = main_products(0, m, [kk])
            last.then_inc(main_done, 1)
            pe.wait_ge(psq_w_ready, 2)
            psq_products(0)
            for s in range(1, SLOTS - SPREAD):
                if s == END_SLOT[1]:
                    pe.wait_ge(ones_set, 3)
                    pe.wait_ge(psq_ready, 1)
                    pe.wait_ge(hidden0_ready, 2)
                slot(s)
                pe_small_layers(s)
            for s in range(SLOTS - SPREAD, SLOTS):
                if s not in DVE_PSQ:
                    psq_products(s)
                pe.wait_ge(cast_ready, s + 1)
                last = main_products(s, 0, range(KC))
                if s == SLOTS - 1:
                    last.then_inc(first_tile_done, 1)
                pe_small_layers(s)
            pe.wait_ge(low_sum_ready, 1)
            nc.tensor.matmul(FLAG_BANK[0:1, 0:1], low_sum[:, :], ones[:, 0:1],
                             start=True, stop=True).then_inc(flag_sum_ready, 1)
            for s in range(SLOTS - SPREAD, SLOTS):
                main_products(s, 1, range(KC)).then_inc(main_done, 1)
            pe_l1(pe, 2, 3)
            pe_l2(pe, 2, 3)
            pe_l3(pe, 2, 3)

            pe.wait_ge(flag_ready, 1)
            general = pe.value_load(flag[0:1, 0:1], min_val=0, max_val=1)
            with pe.If(general == 1):
                pe.sem_inc(g_chunk_done, 1)
                banks_zeroed, loads = 0, 0
                for piece, (n, _, per) in enumerate(PIECES):
                    t = len(PIECES) + piece + 1
                    banks_zeroed += per * MT + 2
                    pe.wait_ge(g_zeroed, banks_zeroed)
                    with pe.Fori(0, NCH) as c:
                        pe.wait_ge(g_landed, c * (16 * (per + 1)) + (loads + 16 * (per + 1)))
                        pe.wait_ge(g_psq_w_ready, c + (NCH * piece + 1))
                        for which in range(per):
                            for kk in range(KC):
                                for m in range(MT):
                                    target = bank[2 * m + which] if piece == 0 else bank[(4, 0)[piece - 1] + m]
                                    nc.tensor.matmul(target[:, :], w_raw[:, 0, kk, m * P:(m + 1) * P],
                                                     x_raw[:, which, kk, :], start=False, stop=False,
                                                     skip_group_check=True)
                                last = nc.tensor.matmul(PSQ_BANK[piece][0:1, :], psq_slow[:, kk:kk + 1],
                                                        x_raw[:, which, kk, :], start=False, stop=False,
                                                        skip_group_check=True)
                        last.then_inc(g_chunk_done, 1)
                    loads += 16 * (per + 1) * NCH
                    pe.wait_ge(g_chunk_done, NCH * (piece + 1) + 1)
                    pe.sem_inc(g_piece_done, 1)
                    pe_l1(pe, piece, t)
                    pe_l2(pe, piece, t)
                    pe_l3(pe, piece, t)


def kernel(r_wfts, r_bfts, r_stm, L0_rec_ft_w, L0_rec_ft_b, L0_rec_l1_w, L0_rec_l1_b, L0_rec_l2_w,
           L0_rec_l2_b, L0_rec_l3_w, L0_rec_l3_b):
    import numpy as np
    import concourse.bacc as bacc
    from concourse.bass_utils import run_bass_kernel_spmd

    def feature_blocks(a):
        a = np.asarray(a)
        return a.reshape(a.shape[0], NCH, KC, P).transpose(1, 3, 2, 0)

    white, black = feature_blocks(r_wfts), feature_blocks(r_bfts)
    x = np.empty((SLOTS, P, KC, COLS), np.float32)
    for (n, row, per), s in zip(PIECES, FIRST_BLOCK):
        if per == 2:
            x[s:s + 2 * NCH:2] = white[..., row:row + n]
            x[s + 1:s + 2 * NCH:2] = black[..., row:row + n]
        else:
            x[s:s + NCH, :, :, 0:n] = white[..., row:row + n]
            x[s:s + NCH, :, :, n:2 * n] = black[..., row:row + n]
    ft_w = np.asarray(L0_rec_ft_w)
    w = np.ascontiguousarray(feature_blocks(ft_w[0:HALF]))
    consts = np.zeros((P, C_ALL), np.float32)
    consts[:, C_FTB:C_FTB + MT] = np.asarray(L0_rec_ft_b)[0:HALF].reshape(MT, P).T
    consts[:, C_W1:C_B1] = np.asarray(L0_rec_l1_w).T.reshape(2 * MT, P, HID).transpose(1, 0, 2).reshape(P, -1)
    consts[0, C_B1:C_W2] = np.tile(np.asarray(L0_rec_l1_b), BLOCKS)
    for q in range(BLOCKS):
        units = slice(q * HID, (q + 1) * HID)
        consts[units, C_W2 + q * HID:C_W2 + (q + 1) * HID] = np.asarray(L0_rec_l2_w).T
        consts[units, C_W3 + q] = np.asarray(L0_rec_l3_w)[0]
    consts[0, C_B2:C_W3] = np.tile(np.asarray(L0_rec_l2_b), BLOCKS)
    consts[0, C_B3:C_BP] = np.asarray(L0_rec_l3_b)[0]
    consts[0, C_BP] = np.asarray(L0_rec_ft_b)[HALF]
    consts[:, C_WP:C_ALL] = ft_w[HALF].reshape(NK, P).T

    nc = bacc.Bacc("TRN2", target_bir_lowering=False, num_devices=1)
    arrays = {"x": x, "w": w, "consts": consts, "stm": np.ascontiguousarray(np.asarray(r_stm).reshape(BATCH))}
    args = [nc.dram_tensor(name, a.shape, F32, kind="ExternalInput").ap() for name, a in arrays.items()]
    out = nc.dram_tensor("out", (BATCH, 1), F32, kind="ExternalOutput").ap()
    build(nc, *args, out)
    return run_bass_kernel_spmd(nc, [arrays], core_ids=[0]).results[0]["out"]
```
